# Optimizing a Trainium2 kernel written in Bass

```python
import numpy as np
import jax
import jax.numpy as jnp

def _softmax(x, axis=-1):
    return jax.nn.softmax(x, axis=axis)

def _gelu(x):
    return jax.nn.gelu(x, approximate=True)

def _silu(x):
    return jax.nn.silu(x)

def _sigmoid(x):
    return jax.nn.sigmoid(x)

def _layernorm(x, axis=-1, eps=1e-05):
    m = jnp.mean(x, axis=axis, keepdims=True)
    v = jnp.var(x, axis=axis, keepdims=True)
    return (x - m) / jnp.sqrt(v + eps)

def _scatter_add(tgt, idx, src, axis=0):
    return tgt.at[idx].add(src)

def _segment_sum(src, seg, n):
    return jax.ops.segment_sum(src, seg, n)
kernel_name = 'mk_cond_seq_d2_seqx_r2_caf0f7'

def setup_inputs(seed: int=0):
    np.random.seed(seed)
    _w = jnp.asarray

    def _rec_inputs():
        import jax
        import jax.numpy as jnp
        _rk = jax.random.key(seed)
        x = 7.22e-05 + 1 * jax.random.normal(jax.random.fold_in(_rk, 1), (16, 512, 512), jnp.float32)
        _lenS = 512 - jax.random.randint(jax.random.fold_in(_rk, 7), (16,), 0, max(1, 512 // 4) + 1, jnp.int32)
        _lenS2 = 512 - jax.random.randint(jax.random.fold_in(_rk, 8), (16,), 0, max(1, 512 // 4) + 1, jnp.int32)
        cond_2048 = 0.00386106 + 1.00199 * jax.random.normal(jax.random.fold_in(_rk, 11), (16, 1024), jnp.float32)
        _validS = jnp.arange(512)[None, :] < _lenS[:, None]
        _validS2 = jnp.arange(512)[None, :] < _lenS2[:, None]
        _causal = jnp.tril(jnp.ones((512, 512), dtype=bool))
        mask_BxS_ff1 = jnp.where(jnp.ones((16, 512), dtype=bool), 1.0, 0.0).astype(jnp.float32)
        mask_BxSx1_fk1 = jnp.where(jnp.ones((16, 512, 1), dtype=bool), 1.0, 0.0).astype(jnp.float32)
        return (x, cond_2048, mask_BxS_ff1, mask_BxSx1_fk1)
    x, cond_2048, mask_BxS_ff1, mask_BxSx1_fk1 = _rec_inputs()

    def _L0_cond_setup():
        import jax, jax.numpy as jnp
        import numpy as np
        B, T, D, H, TE = (8, 512, 512, 16, 1024)
        LN_EPS = 1e-05

        def layer_norm(x, w, b):
            m = jnp.mean(x, axis=-1, keepdims=True)
            v = jnp.var(x, axis=-1, keepdims=True)
            return (x - m) / jnp.sqrt(v + LN_EPS) * w + b
        key = jax.random.key(seed)
        ks = jax.random.split(key, 8)
        s = lambda k, sh: jax.random.normal(k, sh, jnp.float32) * 0.02
        return dict(x=jax.random.normal(ks[0], (B, T, D), jnp.float32), emb=jax.random.normal(ks[1], (B, TE), jnp.float32), src_mask=jnp.ones((B, T), jnp.float32), norm_w=jnp.ones((D,), jnp.float32), norm_b=jnp.zeros((D,), jnp.float32), q_w=s(ks[2], (D, D)), q_b=jnp.zeros((D,), jnp.float32), k_w=s(ks[3], (D, D)), k_b=jnp.zeros((D,), jnp.float32), v_w=s(ks[4], (D, D)), v_b=jnp.zeros((D,), jnp.float32), emb_w=s(ks[5], (TE, 2 * D)), emb_b=jnp.zeros((2 * D,), jnp.float32), sb_norm_w=jnp.ones((D,), jnp.float32), sb_norm_b=jnp.zeros((D,), jnp.float32), out_w=s(ks[6], (D, D)), out_b=jnp.zeros((D,), jnp.float32))
    _L0_cond_all = _L0_cond_setup()
    _L0_cond_in = {k: v for k, v in _L0_cond_all.items() if k in ('norm_w', 'norm_b', 'q_w', 'q_b', 'k_w', 'k_b', 'v_w', 'v_b', 'emb_w', 'emb_b', 'sb_norm_w', 'sb_norm_b', 'out_w', 'out_b')}
    del _L0_cond_all

    def _L1_cond_setup():
        import jax, jax.numpy as jnp
        import numpy as np
        B, T, D, H, TE = (4, 1024, 512, 8, 1024)
        EPS = 1e-05

        def _ln(x, w, b):
            m = jnp.mean(x, axis=-1, keepdims=True)
            v = jnp.mean((x - m) ** 2, axis=-1, keepdims=True)
            return (x - m) * jax.lax.rsqrt(v + EPS) * w + b
        key = jax.random.key(seed)
        ks = jax.random.split(key, 16)
        s = 0.02
        inp = {'x': jax.random.normal(ks[0], (B, T, D), jnp.float32), 'emb': jax.random.normal(ks[1], (B, TE), jnp.float32), 'src_mask': (jax.random.uniform(ks[2], (B, T, 1)) > 0.2).astype(jnp.float32), 'num_head': H, 'ln_w': jnp.ones((D,), jnp.float32), 'ln_b': jnp.zeros((D,), jnp.float32), 'Wq': jax.random.normal(ks[3], (D, D), jnp.float32) * s, 'bq': jnp.zeros((D,), jnp.float32), 'Wk': jax.random.normal(ks[4], (D, D), jnp.float32) * s, 'bk': jnp.zeros((D,), jnp.float32), 'Wv': jax.random.normal(ks[5], (D, D), jnp.float32) * s, 'bv': jnp.zeros((D,), jnp.float32), 'W_emb': jax.random.normal(ks[6], (TE, 2 * D), jnp.float32) * s, 'b_emb': jnp.zeros((2 * D,), jnp.float32), 'ln2_w': jnp.ones((D,), jnp.float32), 'ln2_b': jnp.zeros((D,), jnp.float32), 'W_out': jax.random.normal(ks[7], (D, D), jnp.float32) * s, 'b_out': jnp.zeros((D,), jnp.float32)}
        return inp
    _L1_cond_all = _L1_cond_setup()
    _L1_cond_in = {k: v for k, v in _L1_cond_all.items() if k in ('ln_w', 'ln_b', 'Wq', 'bq', 'Wk', 'bk', 'Wv', 'bv', 'W_emb', 'b_emb', 'ln2_w', 'ln2_b', 'W_out', 'b_out')}
    del _L1_cond_all
    return {'x': x, 'cond_2048': cond_2048, 'mask_BxS_ff1': mask_BxS_ff1, 'mask_BxSx1_fk1': mask_BxSx1_fk1, 'L0_cond_norm_w': _L0_cond_in['norm_w'], 'L0_cond_norm_b': _L0_cond_in['norm_b'], 'L0_cond_q_w': _L0_cond_in['q_w'], 'L0_cond_q_b': _L0_cond_in['q_b'], 'L0_cond_k_w': _L0_cond_in['k_w'], 'L0_cond_k_b': _L0_cond_in['k_b'], 'L0_cond_v_w': _L0_cond_in['v_w'], 'L0_cond_v_b': _L0_cond_in['v_b'], 'L0_cond_emb_w': _L0_cond_in['emb_w'], 'L0_cond_emb_b': _L0_cond_in['emb_b'], 'L0_cond_sb_norm_w': _L0_cond_in['sb_norm_w'], 'L0_cond_sb_norm_b': _L0_cond_in['sb_norm_b'], 'L0_cond_out_w': _L0_cond_in['out_w'], 'L0_cond_out_b': _L0_cond_in['out_b'], 'L1_cond_ln_w': _L1_cond_in['ln_w'], 'L1_cond_ln_b': _L1_cond_in['ln_b'], 'L1_cond_Wq': _L1_cond_in['Wq'], 'L1_cond_bq': _L1_cond_in['bq'], 'L1_cond_Wk': _L1_cond_in['Wk'], 'L1_cond_bk': _L1_cond_in['bk'], 'L1_cond_Wv': _L1_cond_in['Wv'], 'L1_cond_bv': _L1_cond_in['bv'], 'L1_cond_W_emb': _L1_cond_in['W_emb'], 'L1_cond_b_emb': _L1_cond_in['b_emb'], 'L1_cond_ln2_w': _L1_cond_in['ln2_w'], 'L1_cond_ln2_b': _L1_cond_in['ln2_b'], 'L1_cond_W_out': _L1_cond_in['W_out'], 'L1_cond_b_out': _L1_cond_in['b_out']}

def reference(x, cond_2048, mask_BxS_ff1, mask_BxSx1_fk1, L0_cond_norm_w, L0_cond_norm_b, L0_cond_q_w, L0_cond_q_b, L0_cond_k_w, L0_cond_k_b, L0_cond_v_w, L0_cond_v_b, L0_cond_emb_w, L0_cond_emb_b, L0_cond_sb_norm_w, L0_cond_sb_norm_b, L0_cond_out_w, L0_cond_out_b, L1_cond_ln_w, L1_cond_ln_b, L1_cond_Wq, L1_cond_bq, L1_cond_Wk, L1_cond_bk, L1_cond_Wv, L1_cond_bv, L1_cond_W_emb, L1_cond_b_emb, L1_cond_ln2_w, L1_cond_ln2_b, L1_cond_W_out, L1_cond_b_out):
    import jax
    import jax.numpy as jnp

    def _L0_cond_ref(x, emb, src_mask, norm_w, norm_b, q_w, q_b, k_w, k_b, v_w, v_b, emb_w, emb_b, sb_norm_w, sb_norm_b, out_w, out_b):
        import jax, jax.numpy as jnp
        import numpy as np
        B, T, D, H, TE = (8, 512, 512, 16, 1024)
        LN_EPS = 1e-05

        def layer_norm(x, w, b):
            m = jnp.mean(x, axis=-1, keepdims=True)
            v = jnp.var(x, axis=-1, keepdims=True)
            return (x - m) / jnp.sqrt(v + LN_EPS) * w + b
        Bx, Tx, Dx = x.shape
        xn = layer_norm(x, norm_w, norm_b)
        q = (xn @ q_w + q_b).reshape(Bx, Tx, H, -1)
        k = (xn @ k_w + k_b).reshape(Bx, Tx, H, -1)
        att = jnp.einsum('bnhl,bmhl->bnmh', q, k)
        mask = src_mask.reshape(Bx, 1, Tx, 1)
        att = att + (1.0 - mask) * -1000000.0
        att = jax.nn.softmax(att, axis=2)
        v = ((xn @ v_w + v_b) * src_mask[:, :, None]).reshape(Bx, Tx, H, -1)
        y = jnp.einsum('bnmh,bmhl->bnhl', att, v).reshape(Bx, Tx, Dx)
        e = jax.nn.silu(emb) @ emb_w + emb_b
        scale, shift = jnp.split(e[:, None, :], 2, axis=2)
        h = layer_norm(y, sb_norm_w, sb_norm_b) * (1.0 + scale) + shift
        h = jax.nn.silu(h) @ out_w + out_b
        return x + h

    def _L1_cond_ref(x, emb, src_mask, num_head, ln_w, ln_b, Wq, bq, Wk, bk, Wv, bv, W_emb, b_emb, ln2_w, ln2_b, W_out, b_out):
        import jax, jax.numpy as jnp
        import numpy as np
        B, T, D, H, TE = (4, 1024, 512, 8, 1024)
        EPS = 1e-05

        def _ln(x, w, b):
            m = jnp.mean(x, axis=-1, keepdims=True)
            v = jnp.mean((x - m) ** 2, axis=-1, keepdims=True)
            return (x - m) * jax.lax.rsqrt(v + EPS) * w + b
        b, t, d = x.shape
        h = num_head
        dh = d // h
        xn = _ln(x, ln_w, ln_b)
        q = xn @ Wq + bq
        k = xn @ Wk + bk + (1.0 - src_mask) * -1000000.0
        q = jax.nn.softmax(q.reshape(b, t, h, dh), axis=-1)
        k = jax.nn.softmax(k.reshape(b, t, h, dh), axis=1)
        v = ((xn @ Wv + bv) * src_mask).reshape(b, t, h, dh)
        att = jnp.einsum('bnhd,bnhl->bhdl', k, v)
        y = jnp.einsum('bnhd,bhdl->bnhl', q, att).reshape(b, t, d)
        emb_out = (jax.nn.silu(emb) @ W_emb + b_emb)[:, None, :]
        scale, shift = jnp.split(emb_out, 2, axis=2)
        hh = _ln(y, ln2_w, ln2_b) * (1.0 + scale) + shift
        hh = jax.nn.silu(hh) @ W_out + b_out
        return x + hh
    x = _L0_cond_ref(x, cond_2048, mask_BxS_ff1, L0_cond_norm_w, L0_cond_norm_b, L0_cond_q_w, L0_cond_q_b, L0_cond_k_w, L0_cond_k_b, L0_cond_v_w, L0_cond_v_b, L0_cond_emb_w, L0_cond_emb_b, L0_cond_sb_norm_w, L0_cond_sb_norm_b, L0_cond_out_w, L0_cond_out_b)
    x = _L1_cond_ref(x, cond_2048, mask_BxSx1_fk1, 8, L1_cond_ln_w, L1_cond_ln_b, L1_cond_Wq, L1_cond_bq, L1_cond_Wk, L1_cond_bk, L1_cond_Wv, L1_cond_bv, L1_cond_W_emb, L1_cond_b_emb, L1_cond_ln2_w, L1_cond_ln2_b, L1_cond_W_out, L1_cond_b_out)
    return x

_drawn_inputs = setup_inputs


def setup_inputs(seed=0):
    import zlib

    import numpy as np

    out = dict(_drawn_inputs(seed))
    spreads = {'L0_cond_norm_w': (1.0, 0.2),
     'L0_cond_norm_b': (0.0, 0.1),
     'L0_cond_q_b': (0.0, 0.1),
     'L0_cond_k_b': (0.0, 0.8),
     'L0_cond_v_b': (0.0, 0.1),
     'L0_cond_emb_b': (0.0, 0.1),
     'L0_cond_sb_norm_w': (1.0, 0.2),
     'L0_cond_sb_norm_b': (0.0, 0.1),
     'L0_cond_out_b': (0.0, 0.1),
     'L1_cond_ln_w': (1.0, 0.2),
     'L1_cond_ln_b': (0.0, 0.1),
     'L1_cond_bq': (0.0, 0.8),
     'L1_cond_bk': (0.0, 0.8),
     'L1_cond_bv': (0.0, 0.1),
     'L1_cond_b_emb': (0.0, 0.1),
     'L1_cond_ln2_w': (1.0, 0.2),
     'L1_cond_ln2_b': (0.0, 0.299),
     'L1_cond_b_out': (0.0, 0.1)}
    factors = {'L1_cond_Wq': 8.0, 'L1_cond_Wk': 8.0}
    for name, (base, spread) in spreads.items():
        noise = np.random.default_rng([zlib.crc32(name.encode()), seed]).standard_normal(out[name].shape)
        drawn = base * np.exp(spread * noise) if base else spread * noise
        out[name] = jnp.asarray(drawn.astype(out[name].dtype))
    for name, factor in factors.items():
        out[name] = (out[name] * factor).astype(out[name].dtype)
    return out
```

```python
from contextlib import ExitStack

import concourse.bass as bass
from concourse import mybir

F32 = mybir.dt.float32
F32R = mybir.dt.float32r
ALU = mybir.AluOpType
ACT = mybir.ActivationFunctionType
AXX = mybir.AxisListType.X

P = 128
T = 512
D = 512
TT = T // P
KT = D // P
DH0 = 32
HG = P // DH0
NG = KT
SLOTS = TT * HG
LAG = 3
H0 = NG * HG
DH1 = 64
H1 = D // DH1
TE = 1024
CT = TE // P
EPS = 1e-5
BIG = 1000000.0
DMA = 16
ROWS_MAX = 98
ROWS_EXP = 100


def by_head(features):
    return features.rearrange("p (j m) -> p m j", j=HG)


def as_by_head(features):
    return features.rearrange("p (m j) -> p m j", j=HG)


def split_weight(dve, raw, row_scale, hi, lo, hi_done, hi_count, lo_done, src=lambda w: w, dst=lambda w: w):
    for kt in range(KT):
        if row_scale is None:
            dve.tensor_copy(dst(hi[:, kt, :]), src(raw[:, kt, :])).then_inc(hi_done, 1)
        else:
            dve.tensor_scalar(dst(hi[:, kt, :]), src(raw[:, kt, :]), row_scale[:, kt:kt + 1], None,
                              ALU.mult).then_inc(hi_done, 1)
    for kt in range(KT):
        dve.wait_ge(hi_done, hi_count + kt + 1)
        high = dst(hi[:, kt, :].bitcast(F32))
        if row_scale is None:
            last = dve.tensor_tensor(dst(lo[:, kt, :]), src(raw[:, kt, :]), high, ALU.subtract)
        else:
            last = dve.scalar_tensor_tensor(out=dst(lo[:, kt, :]), in0=src(raw[:, kt, :]),
                                            scalar=row_scale[:, kt:kt + 1], in1=high,
                                            op0=ALU.mult, op1=ALU.subtract)
    last.then_inc(lo_done, 1)
    return hi_count + KT


def attention_phase(nc, x, mask, mask1, norm_w, norm_b, q_w, q_b, k_w, k_b, v_w, v_b, yT_dram, sums_dram,
                    mb_dram, mb1_dram):
    B = x.shape[0]
    with ExitStack() as ctx:
        def sb(name, shape, dt=F32):
            return ctx.enter_context(nc.sbuf_tensor(name, shape, dt))

        def bank(name):
            return ctx.enter_context(nc.psum_tensor(name, [P, 512], F32))

        def sem(name):
            return ctx.enter_context(nc.semaphore(name))

        w_hi = {n: sb(f"w{n}_hi", [P, KT, D], F32R) for n in "qkv"}
        w_lo = {n: sb(f"w{n}_lo", [P, KT, D], F32R) for n in "qkv"}
        q_stack = sb("q_stack", [P, NG, HG, T], F32R)
        k_stack = sb("k_stack", [P, NG, HG, T], F32R)
        probs = sb("probs", [P, TT, HG, T])
        probs_sum = sb("probs_sum", [P, HG, T])
        xT_hi = sb("xT_hi", [P, KT, T], F32R)
        xT_lo = sb("xT_lo", [P, KT, T], F32R)
        v_sb = sb("v_sb", [P, TT, D])
        x_sb = sb("x_sb", [P, TT, D])
        stage = {n: sb(f"{n}_stage", [P, 2, T], F32R) for n in "qk"}
        y_stage = sb("y_stage", [P, 2, T])
        sums_stage = sb("sums_stage", [P, T])
        negmax = sb("negmax", [P, SLOTS])
        shift = sb("shift", [SLOTS, 2, P], F32R)
        ident = sb("ident", [P, P])
        head_sel = sb("head_sel", [P, NG, DH0])
        small_rows = sb("small_rows", [2 * KT, P])
        small_cols = sb("small_cols", [P, 2 * KT])
        nw, nb = (small_cols[:, KT * i:KT * (i + 1)] for i in range(2))
        bias_cols = sb("bias_cols", [P, 2, NG])
        bias = {n: bias_cols[:, i, :] for i, n in enumerate("qk")}
        raw_bias = probs_sum[:, 0:2, :]
        full_bias = probs_sum[:, 2:4, :]
        v_bias = sb("v_bias", [P, D])
        mask_col = sb("mask_col", [P, TT, B])
        w_raw = {n: probs[:, i, :, :] for i, n in enumerate("qkv")}
        mb_full = probs[0:B, 3, 0, :]
        mb1_full = y_stage[0:B, 1, :]
        mask_full = sums_stage[0:B, :]
        mb = probs[0:B, 3, 1:3, :]
        nb_rep = probs[:, 3, 3, :].rearrange("p (k c) -> p k c", k=KT)
        stats = sb("stats", [P, TT, 6])
        mv = sb("mv", [P, TT, 2])
        var_eps = sb("var_eps", [P, TT])
        rstd = sb("rstd", [P, TT])
        minus_half = sb("minus_half", [P, TT])

        max_bank = [bank(f"max_bank{i}") for i in range(2)]
        exp_bank = [bank(f"exp_bank{i}") for i in range(2)]
        y_bank = bank("y_bank")
        sums_bank = bank("sums_bank")
        work_bank = [bank(f"work_bank{i}") for i in range(2)]

        ident_zero, ident_done = sem("ident_zero"), sem("ident_done")
        small_in, mask_in = sem("small_in"), sem("mask_in")
        w_in = {n: sem(f"w{n}_in") for n in "qkv"}
        consts_set = sem("consts_set")
        cols_made, cols_done = sem("cols_made"), sem("cols_done")
        nb_rep_done = sem("nb_rep_done")
        w_hi_done, w_split = sem("w_hi_done"), sem("w_split")
        bias_made, bias_done = sem("bias_made"), sem("bias_done")
        mb_step, mb_stored = sem("mb_step"), sem("mb_stored")
        x_in, ln_stats = sem("x_in"), sem("ln_stats")
        rstd_done, xhat_done = sem("rstd_done"), sem("xhat_done")
        work_full, work_read = sem("work_full"), sem("work_read")
        hi_done = sem("hi_done")
        stack_in = [sem(f"stack_in{g}") for g in range(NG)]
        shift_hi, shift_in = sem("shift_hi"), [sem(f"shift_in{g}") for g in range(NG)]
        max_full, max_done = sem("max_full"), sem("max_done")
        exp_full, exp_done = sem("exp_full"), sem("exp_done")
        probs_added, pv_done = sem("probs_added"), sem("pv_done")
        v_done, v_added = sem("v_done"), sem("v_added")
        y_read, y_stored = sem("y_read"), [sem(f"y_stored{i}") for i in range(2)]
        sums_full, sums_read, sums_stored = sem("sums_full"), sem("sums_read"), sem("sums_stored")

        def uses_of(g, last):
            u = []
            if not last or g < NG - 2:
                u += ["q", "k"]
            if g == 0:
                u += ["v2"]
            if g == 1 and not last:
                u += [f"x{tt}" for tt in range(TT)]
            if g == NG - 1 and not last:
                u += ["v0"]
            if not last or g < NG - 1:
                u += ["m"]
            if g == 0:
                u += ["v3"]
            if g == NG - 1 and not last:
                u += ["v1"]
            return u

        FIRST_USES = [f"x{tt}" for tt in range(TT)] + ["q0", "k0", "q1", "k1", "v0", "m", "v1"]
        USES = sum(len(uses_of(g, False)) for g in range(NG))
        assert USES % 2 == 0

        QUARTERS = {"q": (0, 1, 2, 3), "k": (4, 5, 6, 7), "v": (8, 9, 10, 11), "v'": (13, 14, 15, 15)}
        SPREAD = {"q": (0, 1, 2, 4), "k": (5, 6, 8, 9)}
        MAX_TURN = 12

        def quarters(g):
            return SPREAD if g == 2 else QUARTERS

        def maxima(k):
            return range(min(k * 3 // 2, SLOTS), min((k + 1) * 3 // 2, SLOTS))

        def exp_of(b, g, k):
            if k >= LAG:
                return b, g, k - LAG
            return (b, g - 1, k - LAG + SLOTS) if g else (b - 1, NG - 1, k - LAG + SLOTS)

        def use(b, g, what, last=False):
            n = len(FIRST_USES) + sum(len(uses_of(h, last)) for h in range(g)) + uses_of(g, last).index(what)
            return n, b * USES + n

        def step_of(b, g):
            return b * NG + g

        STACK_DMAS = 2 * 3 + 1

        block = ctx.enter_context(nc.Block())

        @block.sync
        def _(sp):
            sp.dma_start(x_sb[:, :, :], x[0].rearrange("(t p) d -> p t d", p=P)).then_inc(x_in, DMA)
            for i, src in enumerate((norm_w, norm_b)):
                sp.dma_start(small_rows[KT * i:KT * (i + 1), :], src.rearrange("(t p) -> t p", p=P)
                             ).then_inc(small_in, DMA)
            for dst, src in ((v_bias[:, :], v_b), (raw_bias[:, 0, :], q_b), (raw_bias[:, 1, :], k_b)):
                sp.dma_start(dst, src.partition_broadcast(P)).then_inc(small_in, DMA)
            for n, w in (("q", q_w), ("k", k_w), ("v", v_w)):
                sp.dma_start(w_raw[n], w.rearrange("(t p) n -> p t n", p=P)).then_inc(w_in[n], DMA)
            sp.dma_start(mask_full, mask).then_inc(mask_in, DMA)
            sp.dma_start(mb1_full, mask1).then_inc(mask_in, DMA)
            sp.wait_ge(mb_step, 6)
            sp.dma_start(mb_dram, mb).then_inc(mb_stored, DMA)
            sp.dma_start(mb1_dram, mb1_full).then_inc(mb_stored, DMA)
            sp.wait_ge(mb_stored, 2 * DMA)

            def mask_rows(b, g):
                sp.dma_start(k_stack[96:98, g, :, :].bitcast(F32),
                             mb_dram[b].unsqueeze(1).broadcast_to([2, HG, T])).then_inc(stack_in[g], DMA)

            def stack(n, g):
                parts = {"q": (0, 1, 0), "k": (0, 0, 1)}[n]
                dst = {"q": q_stack, "k": k_stack}[n]
                for row, part in enumerate(parts):
                    sp.dma_start(dst[DH0 * row:DH0 * row + DH0, g, :, :].bitcast(F32),
                                 stage[n][:, part, :].bitcast(F32)).then_inc(stack_in[g], DMA)

            def shift_rows(b, g, count):
                sp.wait_ge(work_read, count)
                for part in range(2):
                    sp.dma_start(q_stack[ROWS_MAX + part:ROWS_MAX + part + 1, g, :, :].bitcast(F32),
                                 shift[:, part, :].bitcast(F32)).then_inc(shift_in[g], DMA)

            sp.wait_ge(consts_set, 2)
            for g in range(2):
                mask_rows(0, g)
                for i, n in enumerate("qk"):
                    sp.wait_ge(work_read, TT + 2 * g + i + 1)
                    stack(n, g)
            shift_rows(0, 0, FIRST_USES.index("m") + 1)

            def step(b, g, last=False, first=False):
                if not last or g < NG - 2:
                    s_b, s_g = (b, g + 2) if g + 2 < NG else (b + 1, g + 2 - NG)
                    if not (first and g + 2 < NG):
                        sp.wait_ge(exp_full, SLOTS * (step_of(b, g) - 1))
                    mask_rows(s_b, s_g)
                if g == 2 and not last:
                    sp.wait_ge(work_full, use(b, 1, f"x{TT - 1}")[1] + 1)
                    if not (type(b) is int and b + 2 >= B):
                        load_x(b + 2)
                if not last or g < NG - 2:
                    sp.wait_ge(work_read, use(b, g, "q", last)[1] + 1)
                    stack("q", s_g)
                if not (first and g == 0):
                    store_y(b, g - 1) if g else store_y(b - 1, NG - 1)
                if not last or g < NG - 2:
                    sp.wait_ge(work_read, use(b, g, "k", last)[1] + 1)
                    stack("k", s_g)
                if g == 0 and not first:
                    store_sums(b - 1)
                if not last or g < NG - 1:
                    n_b, n_g = (b, g + 1) if g + 1 < NG else (b + 1, 0)
                    shift_rows(n_b, n_g, use(b, g, "m", last)[1] + 1)

            def load_x(b):
                sp.dma_start(x_sb[:, :, :], x[b].rearrange("(t p) d -> p t d", p=P)).then_inc(x_in, DMA)

            def store_y(b, g):
                sp.wait_ge(y_read, step_of(b, g) + 1)
                sp.dma_start(yT_dram[b].rearrange("(j g l) t -> g j l t", j=HG, g=NG)[g], y_stage[:, g % 2, :]).then_inc(y_stored[g % 2], DMA)

            def store_sums(b):
                sp.wait_ge(sums_read, b + 1)
                for j in range(HG):
                    sp.dma_start(sums_dram[b][NG * j:NG * j + NG, :], sums_stage[DH0 * j:DH0 * j + NG, :]
                                 ).then_inc(sums_stored, DMA)

            sp.wait_ge(work_full, TT)
            load_x(1)
            for g in range(NG):
                step(0, g, first=True)
            with sp.Fori(1, B - 2) as b:
                for g in range(NG):
                    step(b, g)
            for g in range(NG):
                step(B - 2, g)
            for g in range(NG):
                step(B - 1, g, last=True)
            store_y(B - 1, NG - 1)
            store_sums(B - 1)
            for i in range(2):
                sp.wait_ge(y_stored[i], DMA * B * NG // 2)
            sp.wait_ge(sums_stored, DMA * HG * B)

        @block.gpsimd
        def _(pool):
            pool.memset(minus_half[:, :], -0.5).then_inc(ident_zero, 1)
            pool.memset(ident[:, :], 0.0).then_inc(ident_zero, 1)
            pool.wait_ge(ident_zero, 2)
            pool.affine_select(out=ident[:, :], in_=ident[:, :], compare_op=ALU.not_equal, fill=1.0,
                               base=0, pattern=[[-1, P]], channel_multiplier=1).then_inc(ident_done, 1)

            def add_probs(s, mt, first=False):
                pool.wait_ge(exp_done, SLOTS * s + HG * (mt + 1))
                if mt == 1:
                    if not first:
                        pool.wait_ge(sums_full, s)
                    so_far = probs[:, 0, :, :]
                else:
                    pool.wait_ge(probs_added, (TT - 1) * s + mt - 1)
                    so_far = probs_sum[:, :, :]
                pool.tensor_tensor(probs_sum[:, :, :], so_far, probs[:, mt, :, :], ALU.add
                                   ).then_inc(probs_added, 1)

            def inverse_deviation(b):
                pool.wait_ge(ln_stats, 3 * (b + 1))
                if not (type(b) is int and b == 0):
                    pool.wait_ge(xhat_done, TT * b)
                pool.tensor_tensor(rstd[:, :], var_eps[:, :], minus_half[:, :], ALU.pow).then_inc(rstd_done, 1)

            def step(b, g, first=False, last=False):
                s = step_of(b, g)
                add_probs(s, 1, first)
                add_probs(s, 2)
                if g == 0 and not last:
                    inverse_deviation(b + 1)
                add_probs(s, 3)

            inverse_deviation(0)
            for g in range(NG):
                step(0, g, first=(g == 0))
            with pool.Fori(1, B - 1) as b:
                for g in range(NG):
                    step(b, g)
            for g in range(NG):
                step(B - 1, g, last=True)

        @block.tensor
        def _(pe):
            def three_passes(out, lhs, rhs):
                n = 0
                for kt in range(KT):
                    for a, c in ((0, 0), (0, 1), (1, 0)):
                        last = pe.matmul(out, lhs(a, kt), rhs(c, kt), start=(n == 0), stop=(n == 3 * KT - 1))
                        n += 1
                return last

            wq_parts = {n: (w_hi[n], w_lo[n]) for n in "qkv"}
            xT = (xT_hi, xT_lo)

            def take_bank(n):
                static, number = n
                if static >= 2:
                    pe.wait_ge(work_read, number - 1)
                return work_bank[static % 2][:, :]

            def project_quarter(what, g, out, kt, first, stop):
                for i, (a, c) in enumerate(((0, 0), (0, 1), (1, 0))):
                    if what in "qk":
                        lhs, rhs = wq_parts[what][a][:, kt, g * P:(g + 1) * P], xT[c][:, kt, :]
                    else:
                        lhs, rhs = xT[c][:, kt, g * P:(g + 1) * P], wq_parts["v"][a][:, kt, :]
                    last = pe.matmul(out, lhs, rhs, start=(first and i == 0), stop=(stop and i == 2))
                if stop:
                    last.then_inc(work_full, 1)

            def transpose_x(tt, number):
                out = take_bank(number)
                for kt in range(KT):
                    last = pe.transpose(out[:, kt * P:(kt + 1) * P], x_sb[:, tt, kt * P:(kt + 1) * P], ident[:, :])
                last.then_inc(work_full, 1)

            def max_scores(b, g, m, first=False):
                j, nt = m // TT, m % TT
                if m == 0:
                    pe.wait_ge(stack_in[g], DMA * STACK_DMAS * (b + 1))
                if not (first and m < 2):
                    pe.wait_ge(max_done, SLOTS * step_of(b, g) + m - 1)
                pe.matmul(max_bank[m % 2][:, :], q_stack[0:ROWS_MAX, g, j, nt * P:(nt + 1) * P],
                          k_stack[0:ROWS_MAX, g, j, :], start=True, stop=True).then_inc(max_full, 1)

            def transpose_max(b, g, number):
                out = take_bank(number)
                pe.wait_ge(max_done, SLOTS * (step_of(b, g) + 1))
                pe.transpose(out[0:SLOTS, 0:P], negmax[:, :], ident[:, :]).then_inc(work_full, 1)

            def exp_scores(b, g, k, first=False):
                mt, j = k // HG, k % HG
                if k == 0:
                    pe.wait_ge(shift_in[g], 2 * DMA * (b + 1))
                if not (first and k < 2):
                    pe.wait_ge(exp_done, SLOTS * step_of(b, g) + k - 1)
                pe.matmul(exp_bank[k % 2][:, :], k_stack[0:ROWS_EXP, g, j, mt * P:(mt + 1) * P],
                          q_stack[0:ROWS_EXP, g, j, :], start=True, stop=True).then_inc(exp_full, 1)

            def weigh_values(b, g, mt):
                s = step_of(b, g)
                pe.wait_ge(exp_done, SLOTS * s + HG * (mt + 1))
                pe.wait_ge(v_done, TT * b + mt + 1)
                if mt == 0 and not (type(s) is int and s == 0):
                    pe.wait_ge(y_read, s)
                for j in range(HG):
                    last = pe.matmul(y_bank[DH0 * j:DH0 * (j + 1), :],
                                     v_sb[:, mt, P * j + DH0 * g:P * j + DH0 * (g + 1)],
                                     probs[:, mt, j, :], start=(mt == 0), stop=(mt == TT - 1))
                last.then_inc(pv_done, 1)

            def sum_probs(b, g):
                s = step_of(b, g)
                pe.wait_ge(probs_added, (TT - 1) * (s + 1))
                if g == 0 and not (type(b) is int and b == 0):
                    pe.wait_ge(sums_read, b)
                for j in range(HG):
                    last = pe.matmul(sums_bank[DH0 * j:DH0 * (j + 1), :], head_sel[:, g, :],
                                     probs_sum[:, j, :], start=(g == 0), stop=(g == NG - 1))
                last.then_inc(sums_full, 1)

            pe.wait_ge(ident_done, 1)
            pe.wait_ge(small_in, 5 * DMA)
            pe.transpose(max_bank[0][:, 0:2 * KT], small_rows[:, :], ident[0:2 * KT, 0:2 * KT]).then_inc(cols_made, 1)
            pe.wait_ge(mask_in, 2 * DMA)
            for tt in range(TT):
                last = pe.transpose(max_bank[1][:, tt * B:(tt + 1) * B], mask_full[:, tt * P:(tt + 1) * P],
                                    ident[0:B, 0:B])
            last.then_inc(cols_made, 1)
            pe.wait_ge(cols_done, 1)
            pe.wait_ge(nb_rep_done, 1)
            for n, out in zip("qkv", (exp_bank[0], exp_bank[1], y_bank)):
                pe.wait_ge(w_in[n], DMA)
                for kt in range(KT):
                    last = pe.matmul(out[:, :], nb_rep[:, kt, :], w_raw[n][:, kt, :], start=(kt == 0), stop=(kt == KT - 1))
                last.then_inc(bias_made, 1)

            for i in range(2):
                pe.wait_ge(bias_done, i + 1)
                for g in range(NG):
                    last = pe.transpose(exp_bank[i][:, g * P:(g + 1) * P], full_bias[:, i, g * P:(g + 1) * P], ident[:, :])
                last.then_inc(bias_made, 1)

            for tt in range(TT):
                pe.wait_ge(xhat_done, tt + 1)
                transpose_x(tt, (tt, tt))
            pe.wait_ge(w_split, 3)
            pe.wait_ge(bias_done, 5)
            pe.wait_ge(work_read, TT)
            n = TT
            for g in range(2):
                for what in "qk":
                    out = take_bank((n, n))
                    for kt in range(KT):
                        project_quarter(what, g, out, kt, kt == 0, kt == KT - 1)
                    n += 1
            out = take_bank((n, n))
            for kt in range(KT):
                project_quarter("v", 0, out, kt, kt == 0, kt == KT - 1)
            for m in range(SLOTS):
                max_scores(0, 0, m, first=True)
            transpose_max(0, 0, (n + 1, n + 1))
            out = take_bank((n + 2, n + 2))
            for kt in range(KT):
                project_quarter("v", 1, out, kt, kt == 0, kt == KT - 1)

            def exp_slot(b, g, e, first=False):
                exp_scores(b, g, e, first)
                before = (b, g - 1) if g else (b - 1, NG - 1)
                if e in (6, 10, 14):
                    weigh_values(b, g, (e - 6) // 4)
                if e == 2 and not first:
                    weigh_values(*before, TT - 1)
                if e == 7 and not first:
                    sum_probs(*before)

            def step(b, g, last=False, first=False):
                banks = {}
                has_next = not last or g < NG - 1
                n_b, n_g = (b, g + 1) if g + 1 < NG else (b + 1, 0)
                for k in range(SLOTS):
                    if not (first and g == 0 and k < LAG):
                        exp_slot(*exp_of(b, g, k), first and g == 0)
                    if has_next:
                        for m in maxima(k):
                            max_scores(n_b, n_g, m)
                        if k == MAX_TURN:
                            transpose_max(n_b, n_g, use(b, g, "m", last))
                    for name, slots in quarters(g).items():
                        if name in "qk":
                            if last and g >= NG - 2:
                                continue
                            what, tile, u = name, (g + 2) % NG, name
                        elif g == 0 or (g == NG - 1 and not last):
                            tile = (2 if g == 0 else 0) + (name == "v'")
                            what, u = "v", f"v{tile}"
                        else:
                            continue
                        for kt in range(KT):
                            if slots[kt] != k:
                                continue
                            if name == "q" and kt == 0 and g == 2:
                                pe.wait_ge(work_read, use(b, 1, f"x{TT - 1}")[1] + 1)
                            if kt == 0:
                                banks[name] = take_bank(use(b, g, u, last))
                            project_quarter(what, tile, banks[name], kt, kt == 0, kt == KT - 1)
                    if g == 1 and not last and 8 <= k < 8 + TT:
                        pe.wait_ge(xhat_done, TT * (b + 1) + k - 8 + 1)
                        transpose_x(k - 8, use(b, 1, f"x{k - 8}"))

            for g in range(NG):
                step(0, g, first=True)
            with pe.Fori(1, B - 1) as b:
                for g in range(NG):
                    step(b, g)
            for g in range(NG):
                step(B - 1, g, last=True)
            for e in range(SLOTS - LAG, SLOTS):
                exp_slot(B - 1, NG - 1, e)
            weigh_values(B - 1, NG - 1, TT - 1)
            sum_probs(B - 1, NG - 1)

        @block.scalar
        def _(act):
            def high_of_x(tt, number, count):
                act.wait_ge(work_full, number + 1)
                act.activation(xT_hi[:, :, tt * P:(tt + 1) * P],
                               work_bank[count % 2][:, :].rearrange("p (k t) -> p k t", k=KT),
                               ACT.Copy).then_inc(hi_done, 1)

            def high_of(what, g, number, count):
                act.wait_ge(work_full, number + 1)
                act.activation(stage[what][:, 0, :], work_bank[count % 2][:, :], ACT.Identity,
                               bias=bias[what][:, g:g + 1]).then_inc(hi_done, 1)

            def mask_value(b, mt, number):
                act.wait_ge(work_read, number + 1)
                act.activation(v_sb[:, mt, :], v_sb[:, mt, :], ACT.Copy, scale=mask_scale(b, mt)
                               ).then_inc(v_done, 1)

            def mask_scale(b, mt):
                return mask_col[:, mt, bass.ds(b, 1)]

            def exp(b, g, k, first=False):
                mt, j = k // HG, k % HG
                s = step_of(b, g)
                act.wait_ge(exp_full, SLOTS * s + k + 1)
                if j == 0 and not first:
                    act.wait_ge(pv_done, TT * (s - 1) + mt + 1)
                    act.wait_ge(probs_added, (TT - 1) * (s - 1) + max(mt, 1))
                act.activation(probs[:, mt, j, :], exp_bank[k % 2][:, :], ACT.Exp).then_inc(exp_done, 1)

            def copy_y(b, g):
                s = step_of(b, g)
                act.wait_ge(pv_done, TT * (s + 1))
                if not (type(b) is int and b == 0 and g < 2):
                    act.wait_ge(y_stored[g % 2], DMA * (b * (NG // 2) + g // 2))
                act.activation(y_stage[:, g % 2, :], y_bank[:, :], ACT.Copy).then_inc(y_read, 1)

            def copy_sums(b):
                act.wait_ge(sums_full, NG * (b + 1))
                if not (type(b) is int and b == 0):
                    act.wait_ge(sums_stored, DMA * HG * b)
                act.activation(sums_stage[:, :], sums_bank[:, :], ACT.Copy).then_inc(sums_read, 1)

            for tt in range(TT):
                high_of_x(tt, tt, tt)
            act.wait_ge(bias_done, 5)
            n = TT
            for g in range(2):
                for what in "qk":
                    if g == 1:
                        act.wait_ge(stack_in[0], DMA * STACK_DMAS)
                    high_of(what, g, n, n)
                    n += 1
            act.wait_ge(cols_done, 2)
            mask_value(0, 0, n)
            mask_value(0, 1, n + 2)

            def exp_slot(b, g, e, first=False):
                exp(b, g, e, first)
                if e == 2 and not first:
                    copy_y(*((b, g - 1) if g else (b - 1, NG - 1)))
                if e == 8 and g == 0 and not first:
                    copy_sums(b - 1)

            def step(b, g, last=False, first=False):
                for k in range(SLOTS):
                    if not (first and g == 0 and k < LAG):
                        exp_slot(*exp_of(b, g, k), first and g == 0)
                    for what in "qk":
                        if k == quarters(g)[what][-1] and (not last or g < NG - 2):
                            p_b, p_g = (b, g + 1) if g + 1 < NG else (b + 1, 0)
                            act.wait_ge(stack_in[p_g], DMA * STACK_DMAS * (p_b + 1))
                            static, number = use(b, g, what, last)
                            high_of(what, (g + 2) % NG, number, static)
                    if g == 1 and not last and 8 <= k < 8 + TT:
                        static, number = use(b, 1, f"x{k - 8}")
                        high_of_x(k - 8, number, static)
                    if k == 12 and (g == 0 or (g == NG - 1 and not last)):
                        mt = 2 if g == 0 else 0
                        mask_value(b if g == 0 else b + 1, mt, use(b, g, f"v{mt}", last)[1])
                if g == 0 or (g == NG - 1 and not last):
                    mt = 3 if g == 0 else 1
                    mask_value(b if g == 0 else b + 1, mt, use(b, g, f"v{mt}", last)[1])

            for g in range(NG):
                step(0, g, first=True)
            with act.Fori(1, B - 1) as b:
                for g in range(NG):
                    step(b, g)
            for g in range(NG):
                step(B - 1, g, last=True)
            for e in range(SLOTS - LAG, SLOTS):
                exp_slot(B - 1, NG - 1, e)
            copy_y(B - 1, NG - 1)
            copy_sums(B - 1)

        @block.vector
        def _(dve):
            def statistics_of_x(b):
                dve.wait_ge(x_in, DMA * (b + 1))
                for tt in range(TT):
                    last = dve.bn_stats(stats[:, tt, :], x_sb[:, tt, :])
                last.then_inc(ln_stats, 1)
                dve.wait_ge(ln_stats, 3 * b + 1)
                dve.memset(var_eps[:, :], EPS)
                for tt in range(TT):
                    last = dve.bn_aggr(mv[:, tt, :], stats[:, tt, :])
                last.then_inc(ln_stats, 1)
                dve.wait_ge(ln_stats, 3 * b + 2)
                dve.tensor_tensor(var_eps[:, :], mv[:, :, 1], var_eps[:, :], ALU.add).then_inc(ln_stats, 1)

            def normalise_x(b, tiles):
                dve.wait_ge(rstd_done, b + 1)
                for tt in tiles:
                    dve.tensor_scalar(x_sb[:, tt, :], x_sb[:, tt, :], mv[:, tt, 0:1], rstd[:, tt:tt + 1],
                                      ALU.subtract, ALU.mult).then_inc(xhat_done, 1)

            def low_of_x(tt, static, hi_count):
                dve.wait_ge(hi_done, hi_count)
                cols = slice(tt * P, (tt + 1) * P)
                dve.tensor_tensor(xT_lo[:, :, cols], work_bank[static % 2][:, :].rearrange("p (k t) -> p k t", k=KT),
                                  xT_hi[:, :, cols].bitcast(F32), ALU.subtract).then_inc(work_read, 1)

            def low_of(what, g, static, hi_count):
                dve.wait_ge(hi_done, hi_count)
                dve.scalar_tensor_tensor(out=stage[what][:, 1, :], in0=work_bank[static % 2][:, :],
                                         scalar=bias[what][:, g:g + 1], in1=stage[what][:, 0, :].bitcast(F32),
                                         op0=ALU.add, op1=ALU.subtract).then_inc(work_read, 1)

            def add_value_bias(b, mt, static, number):
                dve.wait_ge(work_full, number + 1)
                if not (type(b) is int and b == 0):
                    dve.wait_ge(pv_done, TT * (step_of(b, 0) - 1) + mt + 1)
                dve.tensor_tensor(v_sb[:, mt, :], work_bank[static % 2][:, :], v_bias[:, :], ALU.add
                                  ).then_inc(work_read, 1)

            def maximum(b, g, m):
                dve.wait_ge(max_full, SLOTS * step_of(b, g) + m + 1)
                dve.tensor_reduce(negmax[:, m:m + 1], max_bank[m % 2][:, :], AXX, ALU.max, negate=True
                                  ).then_inc(max_done, 1)

            def split_shift(b, g, static, number):
                s = step_of(b, g)
                dve.wait_ge(work_full, number + 1)
                if not (type(s) is int and s == 0):
                    p_b, p_g = (b, g - 1) if g else (b - 1, NG - 1)
                    dve.wait_ge(shift_in[p_g], 2 * DMA * (p_b + 1))
                dve.tensor_copy(shift[:, 0, :], work_bank[static % 2][0:SLOTS, 0:P]).then_inc(shift_hi, 1)
                dve.wait_ge(shift_hi, s + 1)
                dve.tensor_tensor(shift[:, 1, :], work_bank[static % 2][0:SLOTS, 0:P],
                                  shift[:, 0, :].bitcast(F32), ALU.subtract).then_inc(work_read, 1)

            dve.memset(q_stack[96:128, :, :, :].bitcast(F32), 1.0).then_inc(consts_set, 1)
            dve.memset(k_stack[96:128, :, :, :].bitcast(F32), 1.0).then_inc(consts_set, 1)
            dve.memset(head_sel[:, :, :], 0.0).then_inc(consts_set, 1)
            dve.wait_ge(consts_set, 3)
            for g in range(NG):
                last = dve.memset(head_sel[:, g, g:g + 1], 1.0)
            last.then_inc(consts_set, 1)
            dve.memset(nb_rep, 0.0).then_inc(consts_set, 1)
            dve.wait_ge(cols_made, 1)
            dve.tensor_copy(small_cols[:, :], max_bank[0][:, 0:2 * KT]).then_inc(cols_done, 1)
            statistics_of_x(0)
            normalise_x(0, range(TT))
            dve.wait_ge(cols_made, 2)
            dve.tensor_copy(mask_col[:, :, :], max_bank[1][:, 0:TT * B].rearrange("p (t b) -> p t b", t=TT)
                            ).then_inc(cols_done, 1)
            dve.wait_ge(mask_in, 2 * DMA)
            dve.tensor_scalar(mb_full, mask_full, -1.0, 1.0, ALU.mult, ALU.add).then_inc(mb_step, 1)
            dve.wait_ge(mb_step, 1)
            dve.tensor_scalar(mb_full, mb_full, -BIG, None, ALU.mult).then_inc(mb_step, 1)
            dve.wait_ge(mb_step, 2)
            dve.tensor_copy(mb[:, 0, :].bitcast(F32R), mb_full).then_inc(mb_step, 1)
            dve.wait_ge(mb_step, 3)
            dve.tensor_tensor(mb[:, 1, :].bitcast(F32R), mb_full, mb[:, 0, :], ALU.subtract).then_inc(mb_step, 1)
            dve.tensor_scalar(mb1_full, mb1_full, -1.0, 1.0, ALU.mult, ALU.add).then_inc(mb_step, 1)
            dve.wait_ge(mb_step, 5)
            dve.tensor_scalar(mb1_full, mb1_full, -BIG, None, ALU.mult).then_inc(mb_step, 1)
            dve.wait_ge(cols_done, 1)
            dve.wait_ge(consts_set, 5)
            for kt in range(KT):
                last = dve.tensor_scalar(nb_rep[:, kt, :], nb_rep[:, kt, :], nb[:, kt:kt + 1], None, ALU.add)
            last.then_inc(nb_rep_done, 1)
            count = 0
            for n in "qkv":
                dve.wait_ge(w_in[n], DMA)
                count = split_weight(dve, w_raw[n], nw, w_hi[n], w_lo[n], w_hi_done, count, w_split,
                                     **(dict(src=by_head, dst=as_by_head) if n in "qk" else {}))
            dve.wait_ge(small_in, 5 * DMA)
            for i in range(2):
                dve.wait_ge(bias_made, i + 1)
                dve.tensor_tensor(as_by_head(full_bias[:, i, :]), by_head(exp_bank[i][:, :]), by_head(raw_bias[:, i, :]),
                                  ALU.add).then_inc(bias_done, 1)
            dve.wait_ge(bias_made, 3)
            dve.tensor_tensor(v_bias[:, :], y_bank[:, :], v_bias[:, :], ALU.add).then_inc(bias_done, 1)
            for i in range(2):
                dve.wait_ge(bias_made, 4 + i)
                dve.tensor_copy(bias_cols[:, i, :], exp_bank[i][:, :].rearrange("p (g c) -> p g c", g=NG)[:, :, 0]
                                ).then_inc(bias_done, 1)
            dve.wait_ge(bias_done, 5)
            for tt in range(TT):
                low_of_x(tt, tt, tt + 1)
            n = TT
            for g in range(2):
                for what in "qk":
                    low_of(what, g, n, n + 1)
                    n += 1
            add_value_bias(0, 0, n, n)
            for m in range(SLOTS):
                maximum(0, 0, m)
            split_shift(0, 0, n + 1, n + 1)
            add_value_bias(0, 1, n + 2, n + 2)

            HIGHS = 2 * NG + TT

            def high_count(b, g, i):
                return TT + 4 + HIGHS * b + (2 * g + (TT if g > 1 else 0)) + i + 1

            def step(b, g, last=False):
                has_next = not last or g < NG - 1
                n_b, n_g = (b, g + 1) if g + 1 < NG else (b + 1, 0)
                for k in range(SLOTS):
                    if has_next:
                        for m in maxima(k):
                            maximum(n_b, n_g, m)
                    for i, what in enumerate("qk"):
                        if k == quarters(g)[what][-1] + 1 and (not last or g < NG - 2):
                            low_of(what, (g + 2) % NG, use(b, g, what, last)[0], high_count(b, g, i))
                    if g == 1 and not last and 3 <= k < 3 + TT:
                        normalise_x(b + 1, [k - 3])
                    if g == 1 and not last and 9 <= k < 9 + TT:
                        low_of_x(k - 9, use(b, 1, f"x{k - 9}")[0], high_count(b, 1, 2 + k - 9))
                    if k == 11 and (g == 0 or (g == NG - 1 and not last)):
                        mt = 2 if g == 0 else 0
                        add_value_bias(b if g == 0 else b + 1, mt, *use(b, g, f"v{mt}", last))
                    if has_next and k == MAX_TURN:
                        split_shift(n_b, n_g, *use(b, g, "m", last))
                    if g == 0 and not last and k == 13:
                        statistics_of_x(b + 1)
                if g == 0 or (g == NG - 1 and not last):
                    mt = 3 if g == 0 else 1
                    add_value_bias(b if g == 0 else b + 1, mt, *use(b, g, f"v{mt}", last))

            for g in range(NG):
                step(0, g)
            with dve.Fori(1, B - 1) as b:
                for g in range(NG):
                    step(b, g)
            for g in range(NG):
                step(B - 1, g, last=True)


def projection_phase(nc, x, cond, out0_w, out0_b, film0, film1, ln1_w, ln1_b, q_w, q_b, k_w, k_b, v_w, v_b,
                     out1_w, out1_b, mask, yT_dram, sums_dram, mb_dram, out):
    B = x.shape[0]
    with ExitStack() as ctx:
        def sb(name, shape, dt=F32):
            return ctx.enter_context(nc.sbuf_tensor(name, shape, dt))

        def sem(name):
            return ctx.enter_context(nc.semaphore(name))

        WEIGHTS = ("out0", "q", "k", "v", "out1")
        w_hi = {n: sb(f"b_w{n}_hi", [P, KT, D], F32R) for n in WEIGHTS}
        w_lo = {n: sb(f"b_w{n}_lo", [P, KT, D], F32R) for n in WEIGHTS}
        area0 = sb("area0", [P, 4, TT * D])
        area1 = sb("area1", [P, 4, TT * D])

        def tiles(area, i):
            return area[:, i, :].rearrange("p (t n) -> p t n", t=TT)

        yT_sb, x_sb, yn, x1hat = (tiles(area0, i) for i in range(4))
        ekT, ek, v_sb, q_sb = (tiles(area1, i) for i in range(4))
        eqT = ekT
        w_raw = {n: tiles(area0, i) for i, n in enumerate("kvq")}
        w_raw["out1"] = tiles(area0, 3)
        result = sb("result", [P, TT, D])
        w_raw["out0"] = result[:, :, :]
        silu = sb("silu", [P, 2, T])
        cond_rows = silu[0:B, :, :].rearrange("p a n -> p (a n)")
        sT_hi = sb("sT_hi", [P, KT, T], F32R)
        sT_lo = sb("sT_lo", [P, KT, T], F32R)
        x1T_hi = sb("x1T_hi", [P, KT, T], F32R)
        x1T_lo = sb("x1T_lo", [P, KT, T], F32R)
        sums_sb = sb("b_sums", [H0, T])
        mask_bias = sb("mask_bias", [P, T])
        lnb_rep = mask_bias[:, :].rearrange("p (k c) -> p k c", k=KT)
        mask_rows = sums_sb[0:B, :]
        rows = {n: sb(f"row_{n}", [P, D]) for n in ("out0", "q", "v", "out1")}
        att_bd = sb("att_bd", [P, KT, P])
        ident = sb("b_ident", [P, P])
        SMALL = 2 * (TE // P + 2 * KT) + 3 * KT
        small_rows = sb("b_small_rows", [SMALL, P])
        small_cols = sb("b_small_cols", [P, SMALL])
        eb = [small_cols[:, 16 * i:16 * i + 8] for i in range(2)]
        n2w = [small_cols[:, 16 * i + 8:16 * i + 12] for i in range(2)]
        n2b = [small_cols[:, 16 * i + 12:16 * i + 16] for i in range(2)]
        lnw, lnb, k_b_col = (small_cols[:, 32 + 4 * i:36 + 4 * i] for i in range(3))
        k_bias = sb("b_k_bias", [P, NG])
        film_a = [sb(f"film_a{i}", [P, KT, B]) for i in range(2)]
        film_b = [sb(f"film_b{i}", [P, KT, B]) for i in range(2)]
        film_c = sb("film_c", [P, 2, KT, B])
        condT = sb("condT", [P, CT, B])
        mask_col = sb("b_mask_col", [P, TT, B])
        stats = {n: sb(f"stats_{n}", [P, TT, 6]) for n in ("y0", "x1", "y1")}
        mv = {n: sb(f"mv_{n}", [P, TT, 2]) for n in ("y0", "x1", "y1")}
        var_eps = {n: sb(f"var_eps_{n}", [P, TT]) for n in ("y0", "x1", "y1")}
        rstd = {n: sb(f"rstd_{n}", [P, TT]) for n in ("y0", "x1", "y1")}
        minus_half = sb("b_minus_half", [P, TT])
        rinv0 = sb("rinv0", [P, TT, H0])
        kmax = sb("kmax", [P, NG])
        ksum = sb("ksum", [P, NG])
        krec = sb("krec", [P, NG])
        qmax = sb("qmax", [P, TT, H1])
        qsum = sb("qsum", [P, TT, H1])
        qrec = sb("qrec", [P, TT, H1])

        RING = 6
        work_bank = [ctx.enter_context(nc.psum_tensor(f"b_work{i}", [P, 512], F32)) for i in range(RING)]
        sums_bank = ctx.enter_context(nc.psum_tensor("b_sums_bank", [P, 512], F32))
        att_bank = ctx.enter_context(nc.psum_tensor("b_att_bank", [P, 512], F32))

        ident_zero, ident_done = sem("b_ident_zero"), sem("b_ident_done")
        small_in, rows_in, cond_in, mask_in = sem("b_small_in"), sem("rows_in"), sem("cond_in"), sem("b_mask_in")
        emb_in = [sem(f"emb_in{i}") for i in range(2)]
        w_in = {n: sem(f"b_w{n}_in") for n in WEIGHTS}
        cols_made, cols_done = sem("b_cols_made"), sem("b_cols_done")
        cond_act, cond_turned, condT_done = sem("cond_act"), sem("cond_turned"), sem("condT_done")
        film_made, film_step = sem("film_made"), sem("film_step")
        lnb_zero, lnb_rep_done = sem("lnb_zero"), sem("lnb_rep_done")
        bias_made, bias_done = sem("b_bias_made"), sem("b_bias_done")
        w_hi_done, w_split = sem("b_w_hi_done"), sem("b_w_split")
        att_zero = sem("att_zero")
        y_in, x_in, mask_bias_in, stored = sem("y_in"), sem("b_x_in"), sem("mask_bias_in"), sem("b_stored")
        work_full, bank_read = sem("b_work_full"), [sem(f"bank_read{i}") for i in range(RING)]
        sums_turned, rinv0_done = sem("sums_turned"), sem("rinv0_done")
        ln_step = {n: sem(f"ln_step_{n}") for n in ("y0", "x1", "y1")}
        rstd_done = {n: sem(f"rstd_done_{n}") for n in ("y0", "x1", "y1")}
        hat_done = {n: sem(f"hat_done_{n}") for n in ("y0", "x1", "y1")}
        sT_hi_done, sT_lo_done, x1T_hi_done = sem("sT_hi_done"), sem("sT_lo_done"), sem("x1T_hi_done")
        x_biased, result_biased = sem("x_biased"), sem("result_biased")
        k_max_done, k_exp_done, krec_done = sem("k_max_done"), sem("k_exp_done"), sem("krec_done")
        q_max_done, q_shifted, q_exp_done = sem("q_max_done"), sem("q_shifted"), sem("q_exp_done")
        q_sum_done, qrec_done, v_done = sem("q_sum_done"), sem("qrec_done"), sem("b_v_done")
        att_made, att_done = sem("att_made"), sem("att_done")

        ORDER = "KLAVMSHQCJXY"
        TILES = 4
        FIRST = "ASCX"

        def order_of(kind):
            return {"mid": ORDER, "first": "".join(c for c in ORDER if c not in "LM"),
                    "last": "".join(c for c in ORDER if c not in FIRST)}[kind]

        PER_ROW = TILES * len(ORDER)
        assert PER_ROW % RING == 0

        def use(kind, b, what, tile):
            if kind == "start":
                n = TILES * FIRST.index(what) + tile
                return n, n
            if kind == "end":
                n = TILES * (len(order_of("last")) + "LM".index(what)) + tile
            else:
                n = TILES * order_of(kind).index(what) + tile
            n += TILES * len(FIRST) - (0 if kind == "first" else TILES * 2)
            return n, PER_ROW * b + n


        def bank(u):
            return work_bank[u[0] % RING][:, :]

        def reads(b, u):
            return (PER_ROW // RING) * b + u[0] // RING

        def wait_read(eng, kind, b, what, tile):
            u = use(kind, b, what, tile)
            eng.wait_ge(bank_read[u[0] % RING], reads(b, u) + 1)

        def wait_x1T(eng, kind, b):
            for kt in range(KT):
                if kind == "first":
                    wait_read(eng, "start", 0, "X", kt)
                else:
                    wait_read(eng, "mid", b - 1, "X", kt)

        def film_columns(film, kt, b):
            return film[:, kt, bass.ds(b, 1)]

        block = ctx.enter_context(nc.Block())

        @block.sync
        def _(sp):
            def load_y(b):
                sp.dma_start(yT_sb, yT_dram[b].rearrange("(g p) t -> p g t", p=P)).then_inc(y_in, DMA)
                sp.dma_start(sums_sb[:, :], sums_dram[b]).then_inc(y_in, DMA)

            def load_x(b):
                sp.dma_start(x_sb, x[b].rearrange("(t p) d -> p t d", p=P)).then_inc(x_in, DMA)

            def load_mask_bias(b):
                sp.dma_start(mask_bias[:, :], mb_dram[b].partition_broadcast(P)).then_inc(mask_bias_in, DMA)

            sp.dma_start(cond_rows, cond).then_inc(cond_in, DMA)
            at = 0
            for v in (film0[1], film0[2], film0[3], film1[1], film1[2], film1[3], ln1_w, ln1_b, k_b):
                n = v.shape[0] // P
                sp.dma_start(small_rows[at:at + n, :], v.rearrange("(t p) -> t p", p=P)).then_inc(small_in, DMA)
                at += n
            sp.dma_start(mask_rows, mask).then_inc(mask_in, DMA)
            for i, film in enumerate((film0, film1)):
                area = (area0, area1)[i]
                for ct in range(0, CT, 2):
                    sp.dma_start(area[:, ct // 2, :].rearrange("p (c n) -> p c n", c=2),
                                 film[0][ct * P:(ct + 2) * P, :].rearrange("(c p) n -> p c n", p=P)
                                 ).then_inc(emb_in[i], DMA)
            sp.dma_start(w_raw["out0"], out0_w.rearrange("(t p) n -> p t n", p=P)).then_inc(w_in["out0"], DMA)
            for n, v in (("out0", out0_b), ("q", q_b), ("v", v_b), ("out1", out1_b)):
                sp.dma_start(rows[n][:, :], v.partition_broadcast(P)).then_inc(rows_in, DMA)
            sp.wait_ge(film_made, 1)
            for n, w in (("k", k_w), ("v", v_w), ("q", q_w), ("out1", out1_w)):
                sp.dma_start(w_raw[n], w.rearrange("(t p) n -> p t n", p=P)).then_inc(w_in[n], DMA)
            sp.wait_ge(bias_made, 3)
            sp.wait_ge(w_split, len(WEIGHTS))
            load_y(0)
            load_x(0)
            load_mask_bias(0)
            sp.wait_ge(work_full, use("start", 0, "A", TT - 1)[1] + 1)
            load_y(1)

            def iteration(kind, b, more=True):
                if kind != "last":
                    for g in range(NG):
                        wait_read(sp, kind, b, "K", g)
                    load_mask_bias(b + 1)
                    if more:
                        sp.wait_ge(work_full, use(kind, b, "A", TT - 1)[1] + 1)
                        load_y(b + 2)
                if kind != "first":
                    store(kind, b, b - 1)
                if kind != "last":
                    sp.wait_ge(hat_done["x1"], TT * (b + 1))
                    sp.wait_ge(result_biased, b + 1)
                    load_x(b + 1)

            def store(kind, b, row):
                for tt in range(TT):
                    wait_read(sp, kind, b, "M", tt)
                    sp.dma_start(out[row][tt * P:(tt + 1) * P, :], result[:, tt, :]).then_inc(stored, DMA)

            iteration("first", 0)
            with sp.Fori(1, B - 2) as b:
                iteration("mid", b)
            iteration("mid", B - 2, more=False)
            iteration("last", B - 1)
            store("end", B - 1, B - 1)
            sp.wait_ge(stored, DMA * TT * B)

        @block.tensor
        def _(pe):
            def take(kind, b, what, tile):
                u = use(kind, b, what, tile)
                if u[0] >= RING:
                    pe.wait_ge(bank_read[u[0] % RING], reads(b, u))
                return bank(u)

            def three_passes(out, lhs, rhs):
                for kt in range(KT):
                    for a, c in ((0, 0), (0, 1), (1, 0)):
                        last = pe.matmul(out, lhs(a, kt), rhs(c, kt), start=(kt == 0 and a + c == 0),
                                         stop=(kt == KT - 1 and a == 1))
                last.then_inc(work_full, 1)

            def weights(n):
                return w_hi[n], w_lo[n]

            x1T, sT = (x1T_hi, x1T_lo), (sT_hi, sT_lo)

            def by_position(kind, b, what, tile, actT, w):
                out = take(kind, b, what, tile)
                three_passes(out, lambda a, kt: actT[a][:, kt, tile * P:(tile + 1) * P],
                             lambda c, kt: w[c][:, kt, :])

            def by_feature(kind, b, what, tile, w, actT):
                out = take(kind, b, what, tile)
                three_passes(out, lambda a, kt: w[a][:, kt, tile * P:(tile + 1) * P],
                             lambda c, kt: actT[c][:, kt, :])

            def turn(kind, b, what, tile, src):
                out = take(kind, b, what, tile)
                for i in range(4):
                    last = pe.transpose(out[:, i * P:(i + 1) * P], src(i), ident[:, :])
                last.then_inc(work_full, 1)

            def A(kind, b, row):
                pe.wait_ge(y_in, 2 * DMA * (row + 1))
                if not (type(row) is int and row == 0):
                    pe.wait_ge(rinv0_done, row)
                for tt in range(TT):
                    turn(kind, b, "A", tt, lambda i: yT_sb[:, i, tt * P:(tt + 1) * P])
                    if tt == 0:
                        for nt in range(TT):
                            last = pe.transpose(sums_bank[:, nt * H0:(nt + 1) * H0], sums_sb[:, nt * P:(nt + 1) * P],
                                                ident[0:H0, 0:H0])
                        last.then_inc(sums_turned, 1)

            def S(kind, b, row):
                pe.wait_ge(hat_done["y0"], TT * (row + 1))
                for kt in range(KT):
                    turn(kind, b, "S", kt, lambda i: yn[:, i, kt * P:(kt + 1) * P])

            def C(kind, b, count):
                pe.wait_ge(sT_lo_done, count)
                for tt in range(TT):
                    by_position(kind, b, "C", tt, sT, weights("out0"))

            def X(kind, b, row):
                pe.wait_ge(hat_done["x1"], TT * (row + 1))
                for kt in range(KT):
                    turn(kind, b, "X", kt, lambda i: x1hat[:, i, kt * P:(kt + 1) * P])

            def K(kind, b):
                wait_x1T(pe, kind, b)
                for g in range(NG):
                    by_feature(kind, b, "K", g, weights("k"), x1T)

            def V(kind, b):
                for tt in range(TT):
                    by_position(kind, b, "V", tt, x1T, weights("v"))

            def H(kind, b):
                pe.wait_ge(k_exp_done, NG * (b + 1))
                for tt in range(TT):
                    turn(kind, b, "H", tt, lambda i: ekT[:, i, tt * P:(tt + 1) * P])

            def Q(kind, b):
                for tt in range(TT):
                    by_position(kind, b, "Q", tt, x1T, weights("q"))

            def attention(kind, b):
                for tt in range(TT):
                    wait_read(pe, kind, b, "H", tt)
                pe.wait_ge(v_done, TT * (b + 1))
                if not (type(b) is int and b == 0):
                    pe.wait_ge(att_done, b)
                for p in range(KT):
                    for tt in range(TT):
                        last = pe.matmul(att_bank[:, p * P:(p + 1) * P], ek[:, tt, p * P:(p + 1) * P],
                                         v_sb[:, tt, p * P:(p + 1) * P], start=(tt == 0), stop=(tt == TT - 1))
                last.then_inc(att_made, 1)

            def J(kind, b):
                pe.wait_ge(q_exp_done, TT * (b + 1))
                for p in range(KT):
                    turn(kind, b, "J", p, lambda i: q_sb[:, i, p * P:(p + 1) * P])

            def Y(kind, b):
                for p in range(KT):
                    wait_read(pe, kind, b, "J", p)
                pe.wait_ge(att_done, b + 1)
                for tt in range(TT):
                    out = take(kind, b, "Y", tt)
                    for p in range(KT):
                        last = pe.matmul(out[:, p * P:(p + 1) * P], eqT[:, p, tt * P:(tt + 1) * P],
                                         att_bd[:, p, :], start=True, stop=True)
                    last.then_inc(work_full, 1)

            def L(kind, b, row):
                pe.wait_ge(hat_done["y1"], TT * (row + 1))
                for kt in range(KT):
                    turn(kind, b, "L", kt, lambda i: yn[:, i, kt * P:(kt + 1) * P])

            def M(kind, b, count):
                pe.wait_ge(sT_lo_done, count)
                for tt in range(TT):
                    by_position(kind, b, "M", tt, sT, weights("out1"))

            pe.wait_ge(ident_done, 1)
            pe.wait_ge(small_in, 9 * DMA)
            pe.transpose(work_bank[0][:, 0:SMALL], small_rows[:, :], ident[0:SMALL, 0:SMALL]).then_inc(cols_made, 1)
            pe.wait_ge(mask_in, DMA)
            for tt in range(TT):
                last = pe.transpose(work_bank[1][:, tt * B:(tt + 1) * B], mask_rows[:, tt * P:(tt + 1) * P], ident[0:B, 0:B])
            last.then_inc(cols_made, 1)
            pe.wait_ge(cond_act, 1)
            for ct in range(CT):
                last = pe.transpose(work_bank[2][:, ct * B:(ct + 1) * B], cond_rows[:, ct * P:(ct + 1) * P], ident[0:B, 0:B])
            last.then_inc(cond_turned, 1)
            pe.wait_ge(condT_done, 1)
            for i in range(2):
                emb = (area0, area1)[i][:, :, :].rearrange("p a (c n) -> p (a c) n", c=2)
                pe.wait_ge(emb_in[i], DMA * CT // 2)
                for dt in range(TE // P):
                    for ct in range(CT):
                        last = pe.matmul(work_bank[3 + i][:, dt * B:(dt + 1) * B], emb[:, ct, dt * P:(dt + 1) * P],
                                         condT[:, ct, :], start=(ct == 0), stop=(ct == CT - 1))
                last.then_inc(film_made, 1)
            pe.wait_ge(cols_done, 2)
            pe.wait_ge(w_in["k"], DMA)
            for g in range(NG):
                for kt in range(KT):
                    last = pe.matmul(work_bank[5][:, g:g + 1], w_raw["k"][:, kt, g * P:(g + 1) * P], lnb[:, kt:kt + 1],
                                     start=(kt == 0), stop=(kt == KT - 1))
            last.then_inc(bias_made, 1)
            pe.wait_ge(lnb_rep_done, 1)
            for i, n in enumerate("vq"):
                pe.wait_ge(w_in[n], DMA)
                for kt in range(KT):
                    last = pe.matmul((att_bank, sums_bank)[i][:, :], lnb_rep[:, kt, :], w_raw[n][:, kt, :],
                                     start=(kt == 0), stop=(kt == KT - 1))
                last.then_inc(bias_made, 1)
            pe.wait_ge(film_step, 2)
            pe.wait_ge(bias_done, 3)
            pe.wait_ge(w_split, len(WEIGHTS))

            A("start", 0, 0)
            S("start", 0, 0)
            C("start", 0, KT)
            X("start", 0, 0)

            def iteration(kind, b):
                K(kind, b)
                if kind != "first":
                    L(kind, b, b - 1)
                if kind != "last":
                    A(kind, b, b + 1)
                V(kind, b)
                if kind != "first":
                    M(kind, b, KT * (2 * b + 1))
                if kind != "last":
                    S(kind, b, b + 1)
                H(kind, b)
                Q(kind, b)
                if kind != "last":
                    C(kind, b, KT * (2 * b + 2))
                attention(kind, b)
                J(kind, b)
                if kind != "last":
                    X(kind, b, b + 1)
                Y(kind, b)

            iteration("first", 0)
            with pe.Fori(1, B - 1) as b:
                iteration("mid", b)
            iteration("last", B - 1)
            L("end", B - 1, B - 1)
            M("end", B - 1, KT * 2 * B)

        @block.scalar
        def _(act):
            def silus(kind, b, what, film, row, count):
                for kt in range(KT):
                    u = use(kind, b, what, kt)
                    act.wait_ge(work_full, u[1] + 1)
                    if not (kind == "start" and kt < 2):
                        act.wait_ge(sT_lo_done, count + kt - 1)
                    act.activation(silu[:, kt % 2, :], bank(u), ACT.Silu, scale=film_columns(film_a[film], kt, row),
                                   bias=film_columns(film_b[film], kt, row)).then_inc(bank_read[u[0] % RING], 1)

            def copies(kind, b, what, dst, last_reader):
                for i in range(4):
                    u = use(kind, b, what, i)
                    act.wait_ge(work_full, u[1] + 1)
                    act.activation(dst(i), bank(u), ACT.Copy
                                   ).then_inc(bank_read[u[0] % RING] if last_reader else x1T_hi_done, 1)

            act.wait_ge(cond_in, DMA)
            act.activation(cond_rows, cond_rows, ACT.Silu).then_inc(cond_act, 1)
            act.wait_ge(film_step, 8)
            silus("start", 0, "S", 0, 0, 0)
            copies("start", 0, "X", lambda i: x1T_hi[:, i, :], False)

            def iteration(kind, b):
                for g in range(NG):
                    act.wait_ge(k_max_done, NG * b + g + 1)
                    act.activation(ekT[:, g, :], ekT[:, g, :], ACT.Exp, bias=kmax[:, g:g + 1],
                                   accum_out=ksum[:, g:g + 1]).then_inc(k_exp_done, 1)
                if kind != "first":
                    silus(kind, b, "L", 1, b - 1, KT * 2 * b)
                for tt in range(TT):
                    wait_read(act, kind, b, "V", tt)
                    act.activation(v_sb[:, tt, :], v_sb[:, tt, :], ACT.Copy, scale=mask_col[:, tt, bass.ds(b, 1)]
                                   ).then_inc(v_done, 1)
                if kind != "last":
                    silus(kind, b, "S", 0, b + 1, KT * (2 * b + 1))
                copies(kind, b, "H", lambda i: ek[:, i, :], True)
                for tt in range(TT):
                    act.wait_ge(q_shifted, TT * b + tt + 1)
                    act.activation(q_sb[:, tt, :], q_sb[:, tt, :], ACT.Exp).then_inc(q_exp_done, 1)
                copies(kind, b, "J", lambda i: eqT[:, i, :], True)
                if kind != "last":
                    copies(kind, b, "X", lambda i: x1T_hi[:, i, :], False)

            iteration("first", 0)
            with act.Fori(1, B - 1) as b:
                iteration("mid", b)
            iteration("last", B - 1)
            silus("end", B - 1, "L", 1, B - 1, KT * (2 * B - 1))

        @block.gpsimd
        def _(pool):
            def inverse_deviation(n, row):
                pool.wait_ge(ln_step[n], 3 * (row + 1))
                pool.tensor_tensor(rstd[n][:, :], var_eps[n][:, :], minus_half[:, :], ALU.pow).then_inc(rstd_done[n], 1)

            def low_of_silu(count):
                for kt in range(KT):
                    pool.wait_ge(sT_hi_done, count + kt + 1)
                    pool.tensor_tensor(sT_lo[:, kt, :], silu[:, kt % 2, :], sT_hi[:, kt, :].bitcast(F32), ALU.subtract
                                       ).then_inc(sT_lo_done, 1)

            def bias_x(row):
                pool.wait_ge(x_in, DMA * (row + 1))
                pool.tensor_tensor(x_sb, x_sb, rows["out0"][:, :].unsqueeze(1).broadcast_to([P, TT, D]), ALU.add
                                   ).then_inc(x_biased, 1)

            def bias_result(row):
                pool.wait_ge(hat_done["x1"], TT * (row + 1))
                if not (type(row) is int and row == 0):
                    pool.wait_ge(stored, DMA * TT * row)
                pool.tensor_tensor(result[:, :, :], x_sb, rows["out1"][:, :].unsqueeze(1).broadcast_to([P, TT, D]),
                                   ALU.add).then_inc(result_biased, 1)

            pool.memset(minus_half[:, :], -0.5).then_inc(ident_zero, 1)
            pool.memset(ident[:, :], 0.0).then_inc(ident_zero, 1)
            pool.wait_ge(ident_zero, 2)
            pool.affine_select(out=ident[:, :], in_=ident[:, :], compare_op=ALU.not_equal, fill=1.0,
                               base=0, pattern=[[-1, P]], channel_multiplier=1).then_inc(ident_done, 1)
            pool.memset(att_bd[:, :, :], 0.0).then_inc(att_zero, 1)
            pool.wait_ge(rows_in, 4 * DMA)
            inverse_deviation("y0", 0)
            bias_x(0)
            low_of_silu(0)
            inverse_deviation("x1", 0)

            def iteration(kind, b):
                if kind != "first":
                    inverse_deviation("y1", b - 1)
                    low_of_silu(KT * 2 * b)
                if kind != "last":
                    inverse_deviation("y0", b + 1)
                    low_of_silu(KT * (2 * b + 1))
                bias_result(b)
                if kind != "last":
                    bias_x(b + 1)
                for tt in range(TT):
                    pool.wait_ge(q_max_done, TT * b + tt + 1)
                    q = q_sb[:, tt, :].rearrange("p (h d) -> p h d", h=H1)
                    pool.tensor_tensor(q, q, qmax[:, tt, :].unsqueeze(2).broadcast_to([P, H1, DH1]), ALU.add
                                       ).then_inc(q_shifted, 1)
                if kind != "last":
                    inverse_deviation("x1", b + 1)

            iteration("first", 0)
            with pool.Fori(1, B - 1) as b:
                iteration("mid", b)
            iteration("last", B - 1)
            inverse_deviation("y1", B - 1)
            low_of_silu(KT * (2 * B - 1))

        @block.vector
        def _(dve):
            def full(u):
                dve.wait_ge(work_full, u[1] + 1)

            def read(u):
                return bank_read[u[0] % RING]

            def statistics(n, row, src, written):
                for tt in range(TT):
                    written(tt)
                    last = dve.bn_stats(stats[n][:, tt, :], src[:, tt, :])
                last.then_inc(ln_step[n], 1)
                dve.wait_ge(ln_step[n], 3 * row + 1)
                dve.memset(var_eps[n][:, :], EPS)
                for tt in range(TT):
                    last = dve.bn_aggr(mv[n][:, tt, :], stats[n][:, tt, :])
                last.then_inc(ln_step[n], 1)
                dve.wait_ge(ln_step[n], 3 * row + 2)
                dve.tensor_tensor(var_eps[n][:, :], mv[n][:, :, 1], var_eps[n][:, :], ALU.add).then_inc(ln_step[n], 1)

            def normalise(n, row, src, dst):
                dve.wait_ge(rstd_done[n], row + 1)
                for tt in range(TT):
                    dve.tensor_scalar(dst[:, tt, :], src[:, tt, :], mv[n][:, tt, 0:1], rstd[n][:, tt:tt + 1],
                                      ALU.subtract, ALU.mult).then_inc(hat_done[n], 1)

            def normalised_heads(kind, b, what, rec, split, order, n, row):
                for tt in range(TT):
                    u = use(kind, b, what, tt)
                    full(u)
                    dve.tensor_tensor(yn[:, tt, :].rearrange(split, **order), bank(u).rearrange(split, **order),
                                      rec(tt), ALU.mult).then_inc(read(u), 1)
                statistics(n, row, yn, lambda tt: wait_read(dve, kind, b, what, tt))

            def A(kind, b, row):
                dve.wait_ge(sums_turned, row + 1)
                dve.reciprocal(rinv0[:, :, :], sums_bank[:, 0:TT * H0].rearrange("p (t h) -> p t h", t=TT)
                               ).then_inc(rinv0_done, 1)
                dve.wait_ge(rinv0_done, row + 1)
                normalised_heads(kind, b, "A",
                                 lambda tt: rinv0[:, tt, :].unsqueeze(2).broadcast_to([P, H0, DH0]),
                                 "p (h l) -> p h l", dict(h=H0), "y0", row)

            def Y(kind, b):
                dve.wait_ge(qrec_done, b + 1)
                normalised_heads(kind, b, "Y",
                                 lambda tt: qrec[:, tt, :].unsqueeze(2).broadcast_to([P, H1, DH1]),
                                 "p (h d) -> p h d", dict(h=H1), "y1", b)

            def highs_of_silu(kind, b, what):
                for kt in range(KT):
                    wait_read(dve, kind, b, what, kt)
                    dve.tensor_copy(sT_hi[:, kt, :], silu[:, kt % 2, :]).then_inc(sT_hi_done, 1)

            def C(kind, b, row):
                dve.wait_ge(x_biased, row + 1)
                for tt in range(TT):
                    u = use(kind, b, "C", tt)
                    full(u)
                    dve.tensor_tensor(x_sb[:, tt, :], bank(u), x_sb[:, tt, :], ALU.add).then_inc(read(u), 1)
                statistics("x1", row, x_sb, lambda tt: wait_read(dve, kind, b, "C", tt))

            def X(kind, b, row):
                for kt in range(KT):
                    u = use(kind, b, "X", kt)
                    dve.wait_ge(x1T_hi_done, KT * row + kt + 1)
                    dve.tensor_tensor(x1T_lo[:, kt, :], bank(u), x1T_hi[:, kt, :].bitcast(F32), ALU.subtract
                                      ).then_inc(read(u), 1)

            def k_tile(kind, b, g):
                u = use(kind, b, "K", g)
                full(u)
                dve.scalar_tensor_tensor(out=ekT[:, g, :], in0=bank(u), scalar=k_bias[:, g:g + 1],
                                         in1=mask_bias[:, :], op0=ALU.add, op1=ALU.add).then_inc(read(u), 1)

            def k_max(kind, b, g):
                wait_read(dve, kind, b, "K", g)
                dve.tensor_reduce(kmax[:, g:g + 1], ekT[:, g, :], AXX, ALU.max, negate=True).then_inc(k_max_done, 1)

            def q_tile(kind, b, tt):
                u = use(kind, b, "Q", tt)
                full(u)
                dve.tensor_tensor(q_sb[:, tt, :], bank(u), rows["q"][:, :], ALU.add).then_inc(read(u), 1)

            def q_max(kind, b, tt):
                wait_read(dve, kind, b, "Q", tt)
                dve.tensor_reduce(qmax[:, tt, :], q_sb[:, tt, :].rearrange("p (h d) -> p h d", h=H1), AXX, ALU.max,
                                  negate=True).then_inc(q_max_done, 1)

            def add_row(kind, b, what, tt, dst, row):
                u = use(kind, b, what, tt)
                full(u)
                dve.tensor_tensor(dst[:, tt, :], bank(u), row, ALU.add).then_inc(read(u), 1)

            def add_result(kind, b, row):
                dve.wait_ge(result_biased, row + 1)
                for tt in range(TT):
                    add_row(kind, b, "M", tt, result, result[:, tt, :])

            dve.wait_ge(cols_made, 1)
            dve.tensor_copy(small_cols[:, :], work_bank[0][:, 0:SMALL]).then_inc(cols_done, 1)
            dve.wait_ge(cols_made, 2)
            dve.tensor_copy(mask_col[:, :, :], work_bank[1][:, 0:TT * B].rearrange("p (t b) -> p t b", t=TT)
                            ).then_inc(cols_done, 1)
            dve.wait_ge(cond_turned, 1)
            dve.tensor_copy(condT[:, :, :], work_bank[2][:, 0:CT * B].rearrange("p (c b) -> p c b", c=CT)
                            ).then_inc(condT_done, 1)
            dve.memset(lnb_rep, 0.0).then_inc(lnb_zero, 1)
            dve.wait_ge(lnb_zero, 1)
            dve.wait_ge(cols_done, 2)
            for kt in range(KT):
                last = dve.tensor_scalar(lnb_rep[:, kt, :], lnb_rep[:, kt, :], lnb[:, kt:kt + 1], None, ALU.add)
            last.then_inc(lnb_rep_done, 1)
            def by_row(column):
                return column.unsqueeze(2).broadcast_to([P, KT, B])

            for i in range(2):
                dve.wait_ge(film_made, i + 1)
                e = work_bank[3 + i][:, 0:2 * KT * B].rearrange("p (c b) -> p c b", b=B)
                dve.tensor_tensor(film_a[i][:, :, :], e[:, 0:KT, :], by_row(eb[i][:, 0:KT]), ALU.add)
                dve.tensor_tensor(film_b[i][:, :, :], e[:, KT:2 * KT, :], by_row(eb[i][:, KT:2 * KT]), ALU.add
                                  ).then_inc(film_step, 1)
            dve.wait_ge(film_step, 2)
            for i in range(2):
                dve.tensor_scalar(film_a[i][:, :, :], film_a[i][:, :, :], 1.0, None, ALU.add).then_inc(film_step, 1)
            dve.wait_ge(film_step, 4)
            for i in range(2):
                dve.tensor_tensor(film_c[:, i, :, :], film_a[i][:, :, :], by_row(n2b[i]), ALU.mult).then_inc(film_step, 1)
            dve.wait_ge(film_step, 6)
            for i in range(2):
                dve.tensor_tensor(film_a[i][:, :, :], film_a[i][:, :, :], by_row(n2w[i]), ALU.mult)
                dve.tensor_tensor(film_b[i][:, :, :], film_b[i][:, :, :], film_c[:, i, :, :], ALU.add
                                  ).then_inc(film_step, 1)
            count = 0
            for n in ("out0", "k", "v", "q", "out1"):
                dve.wait_ge(w_in[n], DMA)
                count = split_weight(dve, w_raw[n], None if n in ("out0", "out1") else lnw, w_hi[n], w_lo[n],
                                     w_hi_done, count, w_split)
            dve.wait_ge(bias_made, 1)
            dve.tensor_tensor(k_bias[:, :], work_bank[5][:, 0:NG], k_b_col, ALU.add).then_inc(bias_done, 1)
            dve.wait_ge(rows_in, 4 * DMA)
            for i, n in enumerate("vq"):
                dve.wait_ge(bias_made, 2 + i)
                dve.tensor_tensor(rows[n][:, :], (att_bank, sums_bank)[i][:, :], rows[n][:, :], ALU.add).then_inc(bias_done, 1)
            dve.wait_ge(bias_done, 3)

            A("start", 0, 0)
            normalise("y0", 0, yn, yn)
            highs_of_silu("start", 0, "S")
            C("start", 0, 0)
            normalise("x1", 0, x_sb, x1hat)
            X("start", 0, 0)

            def iteration(kind, b):
                dve.wait_ge(mask_bias_in, DMA * (b + 1))
                k_tile(kind, b, 0)
                k_tile(kind, b, 1)
                k_max(kind, b, 0)
                if kind != "first":
                    normalise("y1", b - 1, yn, yn)
                for g in range(2, NG):
                    k_tile(kind, b, g)
                    k_max(kind, b, g - 1)
                k_max(kind, b, NG - 1)
                if kind != "first":
                    highs_of_silu(kind, b, "L")
                if kind != "last":
                    A(kind, b, b + 1)
                add_row(kind, b, "V", 0, v_sb, rows["v"][:, :])
                add_row(kind, b, "V", 1, v_sb, rows["v"][:, :])
                if kind != "last":
                    normalise("y0", b + 1, yn, yn)
                add_row(kind, b, "V", 2, v_sb, rows["v"][:, :])
                add_row(kind, b, "V", 3, v_sb, rows["v"][:, :])
                if kind != "first":
                    add_result(kind, b, b - 1)
                if kind != "last":
                    highs_of_silu(kind, b, "S")
                dve.wait_ge(k_exp_done, NG * (b + 1))
                dve.reciprocal(krec[:, :], ksum[:, :]).then_inc(krec_done, 1)
                q_tile(kind, b, 0)
                for tt in range(1, TT):
                    q_tile(kind, b, tt)
                    q_max(kind, b, tt - 1)
                q_max(kind, b, TT - 1)
                if kind != "last":
                    C(kind, b, b + 1)
                dve.wait_ge(att_made, b + 1)
                dve.wait_ge(krec_done, b + 1)
                for half in range(2):
                    at = slice(DH1 * half, DH1 * (half + 1))
                    last = dve.tensor_tensor(att_bd[at, :, at], att_bank[at, :].rearrange("p (k c) -> p k c", k=KT)[:, :, at],
                                             krec[at, :].unsqueeze(2).broadcast_to([DH1, KT, DH1]), ALU.mult)
                last.then_inc(att_done, 1)
                for tt in range(TT):
                    dve.wait_ge(q_exp_done, TT * b + tt + 1)
                    last = dve.tensor_reduce(qsum[:, tt, :], q_sb[:, tt, :].rearrange("p (h d) -> p h d", h=H1), AXX, ALU.add)
                last.then_inc(q_sum_done, 1)
                if kind != "last":
                    normalise("x1", b + 1, x_sb, x1hat)
                dve.wait_ge(q_sum_done, b + 1)
                dve.reciprocal(qrec[:, :, :], qsum[:, :, :]).then_inc(qrec_done, 1)
                if kind != "last":
                    X(kind, b, b + 1)
                Y(kind, b)

            dve.wait_ge(att_zero, 1)
            iteration("first", 0)
            with dve.Fori(1, B - 1) as b:
                iteration("mid", b)
            iteration("last", B - 1)
            normalise("y1", B - 1, yn, yn)
            highs_of_silu("end", B - 1, "L")
            add_result("end", B - 1, B - 1)


_NAMES = ["x", "cond_2048", "mask_BxS_ff1", "mask_BxSx1_fk1", "L0_cond_norm_w", "L0_cond_norm_b", "L0_cond_q_w",
          "L0_cond_q_b", "L0_cond_k_w", "L0_cond_k_b", "L0_cond_v_w", "L0_cond_v_b", "L0_cond_emb_w", "L0_cond_emb_b",
          "L0_cond_sb_norm_w", "L0_cond_sb_norm_b", "L0_cond_out_w", "L0_cond_out_b", "L1_cond_ln_w", "L1_cond_ln_b",
          "L1_cond_Wq", "L1_cond_bq", "L1_cond_Wk", "L1_cond_bk", "L1_cond_Wv", "L1_cond_bv", "L1_cond_W_emb",
          "L1_cond_b_emb", "L1_cond_ln2_w", "L1_cond_ln2_b", "L1_cond_W_out", "L1_cond_b_out"]


def build(nc, i, out):
    B = i["x"].shape[0]
    yT_dram = nc.dram_tensor("yT_scratch", (B, D, T), F32, kind="Internal").ap()
    sums_dram = nc.dram_tensor("sums_scratch", (B, NG * HG, T), F32, kind="Internal").ap()
    mb0_dram = nc.dram_tensor("mask_bias0_scratch", (B, 2, T), F32, kind="Internal").ap()
    mb1_dram = nc.dram_tensor("mask_bias1_scratch", (B, T), F32, kind="Internal").ap()
    mask1 = i["mask_BxSx1_fk1"].rearrange("b t o -> b (t o)")
    attention_phase(nc, i["x"], i["mask_BxS_ff1"], mask1, i["L0_cond_norm_w"], i["L0_cond_norm_b"], i["L0_cond_q_w"],
                    i["L0_cond_q_b"], i["L0_cond_k_w"], i["L0_cond_k_b"], i["L0_cond_v_w"], i["L0_cond_v_b"],
                    yT_dram, sums_dram, mb0_dram, mb1_dram)
    projection_phase(nc, i["x"], i["cond_2048"], i["L0_cond_out_w"], i["L0_cond_out_b"],
                     tuple(i["L0_cond_" + n] for n in ("emb_w", "emb_b", "sb_norm_w", "sb_norm_b")),
                     tuple(i["L1_cond_" + n] for n in ("W_emb", "b_emb", "ln2_w", "ln2_b")),
                     i["L1_cond_ln_w"], i["L1_cond_ln_b"], i["L1_cond_Wq"], i["L1_cond_bq"], i["L1_cond_Wk"],
                     i["L1_cond_bk"], i["L1_cond_Wv"], i["L1_cond_bv"], i["L1_cond_W_out"], i["L1_cond_b_out"],
                     mask1, yT_dram, sums_dram, mb1_dram, out)


def kernel(**inputs):
    import concourse.bacc as bacc
    import numpy as np
    from concourse.bass_utils import run_bass_kernel_spmd

    nc = bacc.Bacc("TRN2", target_bir_lowering=False, num_devices=1)
    arrays, aps = {}, {}
    for name in _NAMES:
        a = np.ascontiguousarray(inputs[name])
        arrays[f"in_{name}"] = a
        aps[name] = nc.dram_tensor(f"in_{name}", a.shape, mybir.dt.from_np(a.dtype), kind="ExternalInput").ap()
    out = nc.dram_tensor("out_x", arrays["in_x"].shape, F32, kind="ExternalOutput").ap()
    build(nc, aps, out)
    r = run_bass_kernel_spmd(nc, [arrays], core_ids=[0])
    return r.results[0]["out_x"]
```

```python
from contextlib import ExitStack

import concourse.bass as bass
from concourse import mybir

F32 = mybir.dt.float32
F32R = mybir.dt.float32r
ALU = mybir.AluOpType
ACT = mybir.ActivationFunctionType
AXX = mybir.AxisListType.X

P = 128
T = 512
D = 512
TT = T // P
KT = D // P
DH0 = 32
HG = P // DH0
NG = KT
SLOTS = TT * HG
LAG = 3
H0 = NG * HG
DH1 = 64
H1 = D // DH1
TE = 1024
CT = TE // P
EPS = 1e-5
BIG = 1000000.0
DMA = 16
ROWS_MAX = 98
ROWS_EXP = 100
B_ROWS = 2 * (TE // P + 2 * KT) + 3 * KT


def by_head(features):
    return features.rearrange("p (j m) -> p m j", j=HG)


def as_by_head(features):
    return features.rearrange("p (m j) -> p m j", j=HG)


def high_of_weight(act, raw, row_scale, hi, hi_done, src=lambda w: w, dst=lambda w: w):
    for kt in range(KT):
        if row_scale is None:
            act.activation(dst(hi[:, kt, :]), src(raw[:, kt, :]), ACT.Copy).then_inc(hi_done, 1)
        else:
            act.activation(dst(hi[:, kt, :]), src(raw[:, kt, :]), ACT.Copy, scale=row_scale[:, kt:kt + 1]
                           ).then_inc(hi_done, 1)


def low_of_weight(dve, raw, row_scale, hi, lo, hi_done, lo_done, src=lambda w: w, dst=lambda w: w):
    for kt in range(KT):
        dve.wait_ge(hi_done, kt + 1)
        high = dst(hi[:, kt, :].bitcast(F32))
        if row_scale is None:
            last = dve.tensor_tensor(dst(lo[:, kt, :]), src(raw[:, kt, :]), high, ALU.subtract)
        else:
            last = dve.scalar_tensor_tensor(out=dst(lo[:, kt, :]), in0=src(raw[:, kt, :]),
                                            scalar=row_scale[:, kt:kt + 1], in1=high,
                                            op0=ALU.mult, op1=ALU.subtract)
    last.then_inc(lo_done, 1)


class Shared:

    def __init__(self, nc, ctx, B):
        def sb(name, shape):
            return ctx.enter_context(nc.sbuf_tensor(name, shape, F32))

        self.ident = sb("ident", [P, P])
        self.film_a = [sb(f"film_a{i}", [P, KT, B]) for i in range(2)]
        self.film_b = [sb(f"film_b{i}", [P, KT, B]) for i in range(2)]
        self.mask1_col = sb("mask1_col", [P, TT, B])
        self.cols = sb("b_cols", [P, B_ROWS])
        self.eb = [self.cols[:, 16 * i:16 * i + 8] for i in range(2)]
        self.n2w = [self.cols[:, 16 * i + 8:16 * i + 12] for i in range(2)]
        self.n2b = [self.cols[:, 16 * i + 12:16 * i + 16] for i in range(2)]
        self.lnw, self.lnb, self.k_b = (self.cols[:, 32 + 4 * i:36 + 4 * i] for i in range(3))


def attention_phase(nc, shared, x, mask, mask1, norm_w, norm_b, q_w, q_b, k_w, k_b, v_w, v_b, cond, films, b_vectors,
                    yT_dram, sums_dram, mb_dram, mb1_dram):
    B = x.shape[0]
    with ExitStack() as ctx:
        def sb(name, shape, dt=F32):
            return ctx.enter_context(nc.sbuf_tensor(name, shape, dt))

        def bank(name):
            return ctx.enter_context(nc.psum_tensor(name, [P, 512], F32))

        def sem(name):
            return ctx.enter_context(nc.semaphore(name))

        w_hi = {n: sb(f"w{n}_hi", [P, KT, D], F32R) for n in "qkv"}
        w_lo = {n: sb(f"w{n}_lo", [P, KT, D], F32R) for n in "qkv"}
        q_stack = sb("q_stack", [P, NG, HG, T], F32R)
        k_stack = sb("k_stack", [P, NG, HG, T], F32R)
        probs = sb("probs", [P, TT, HG, T])
        probs_sum = sb("probs_sum", [P, HG, T])
        xT_hi = sb("xT_hi", [P, KT, T], F32R)
        xT_lo = sb("xT_lo", [P, KT, T], F32R)
        v_sb = sb("v_sb", [P, TT, D])
        x_sb = sb("x_sb", [P, TT, D])
        stage = {n: sb(f"{n}_stage", [P, 2, T], F32R) for n in "qk"}
        y_stage = sb("y_stage", [P, 2, T])
        sums_stage = sb("sums_stage", [P, T])
        negmax = sb("negmax", [P, SLOTS])
        shift = sb("shift", [SLOTS, 2, P], F32R)
        ident = shared.ident
        head_sel = sb("head_sel", [P, NG, DH0])
        small_rows = sb("small_rows", [2 * KT, P])
        small_cols = sb("small_cols", [P, 2 * KT])
        nw, nb = (small_cols[:, KT * i:KT * (i + 1)] for i in range(2))
        bias_cols = sb("bias_cols", [P, 2, NG])
        bias = {n: bias_cols[:, i, :] for i, n in enumerate("qk")}
        v_bias = sb("v_bias", [P, D])
        mask_col = sb("mask_col", [P, TT, B])
        raw_bias = probs_sum[:, 0:2, :]
        full_bias = probs_sum[:, 2:4, :]
        emb = [[part.rearrange("p c n -> p (c n)").rearrange("p (c n) -> p c n", c=2)
                for part in (x_sb[:, :, :], probs[:, 0, :, :], probs[:, 1, :, :], last)]
               for last in (v_sb[:, :, :], probs[:, 2, :, :])]
        cond_rows = v_sb[0:B, 0:2, :].rearrange("p a n -> p (a n)")
        b_rows = v_sb[0:B_ROWS, 2, 0:P]
        ones = y_stage[0:2, 0, :]
        condT = sb("condT", [P, CT, DH0])
        row_sel = sb("row_sel", [P, B])
        film_rows = raw_bias
        film_c = sb("film_c", [P, 2, KT, B])
        w_raw = {n: probs[:, i, :, :] for i, n in enumerate("qkv")}
        mb_full = probs[0:B, 3, 0, :]
        mb1_full = y_stage[0:B, 1, :]
        mask_full = sums_stage[0:B, :]
        mb = probs[0:B, 3, 1:3, :]
        nb_rep = probs[:, 3, 3, :].rearrange("p (k c) -> p k c", k=KT)
        stats = sb("stats", [P, TT, 6])
        mv = sb("mv", [P, TT, 2])
        var_eps = sb("var_eps", [P, TT])
        rstd = sb("rstd", [P, TT])
        minus_half = sb("minus_half", [P, TT])

        max_bank = [bank(f"max_bank{i}") for i in range(2)]
        exp_bank = [bank(f"exp_bank{i}") for i in range(2)]
        y_bank = bank("y_bank")
        sums_bank = bank("sums_bank")
        work_bank = [bank(f"work_bank{i}") for i in range(2)]

        ident_zero, ident_done = sem("ident_zero"), sem("ident_done")
        norm_in, bias_in, mask_in = sem("norm_in"), sem("bias_in"), sem("mask_in")
        cond_in, b_rows_in, emb_in = sem("cond_in"), sem("b_rows_in"), sem("emb_in")
        cond_act, cond_turned, condT_done = sem("cond_act"), sem("cond_turned"), sem("condT_done")
        film_full, film_copied, row_sel_done = sem("film_full"), sem("film_copied"), sem("row_sel_done")
        film_made, film_step = sem("film_made"), sem("film_step")
        ones_set, ones_in, head_sel_zero = sem("ones_set"), sem("ones_in"), sem("head_sel_zero")
        w_in = {n: sem(f"w{n}_in") for n in "qkv"}
        cols_made, cols_done = sem("cols_made"), sem("cols_done")
        nb_rep_done = sem("nb_rep_done")
        w_hi_done, w_split = {n: sem(f"w{n}_hi_done") for n in "qkv"}, sem("w_split")
        bias_made, bias_full, v_bias_done = sem("bias_made"), sem("bias_full"), sem("v_bias_done")
        bias_turned, bias_done = sem("bias_turned"), sem("bias_done")
        mb_step, mb_stored = sem("mb_step"), sem("mb_stored")
        x_in, ln_stats = sem("x_in"), sem("ln_stats")
        rstd_done, xhat_done = sem("rstd_done"), sem("xhat_done")
        work_full, work_read = sem("work_full"), sem("work_read")
        hi_done = sem("hi_done")
        stack_in = [sem(f"stack_in{g}") for g in range(NG)]
        shift_hi, shift_in = sem("shift_hi"), [sem(f"shift_in{g}") for g in range(NG)]
        max_full, max_done = sem("max_full"), sem("max_done")
        exp_full, exp_done = sem("exp_full"), sem("exp_done")
        probs_added, pv_done = sem("probs_added"), sem("pv_done")
        v_done, v_added = sem("v_done"), sem("v_added")
        y_read, y_stored = sem("y_read"), [sem(f"y_stored{i}") for i in range(2)]
        sums_full, sums_read, sums_stored = sem("sums_full"), sem("sums_read"), sem("sums_stored")

        def uses_of(g, last):
            u = []
            if not last or g < NG - 2:
                u += ["q", "k"]
            if g == 0:
                u += ["v2"]
            if g == 1 and not last:
                u += [f"x{tt}" for tt in range(TT - 1)]
            if g == NG - 1 and not last:
                u += ["v0"]
            if not last or g < NG - 1:
                u += ["m"]
            if g == 1 and not last:
                u += [f"x{TT - 1}"]
            if g == 0:
                u += ["v3"]
            if g == NG - 1 and not last:
                u += ["v1"]
            return u

        FIRST_USES = [f"x{tt}" for tt in range(TT)] + ["q0", "k0", "q1", "k1", "m", "v0", "v1"]
        USES = sum(len(uses_of(g, False)) for g in range(NG))
        assert USES % 2 == 0

        QUARTERS = {"q": (0, 1, 2, 3), "k": (4, 5, 6, 7), "v": (8, 9, 10, 11), "v'": (13, 14, 15, 15)}
        X_TURNS = (8, 9, 11, 13)
        MAX_TURN = 12

        def maxima(k):
            return range(min(k * 3 // 2, SLOTS), min((k + 1) * 3 // 2, SLOTS))

        def exp_of(b, g, k):
            if k >= LAG:
                return b, g, k - LAG
            return (b, g - 1, k - LAG + SLOTS) if g else (b - 1, NG - 1, k - LAG + SLOTS)

        def use(b, g, what, last=False):
            n = len(FIRST_USES) + sum(len(uses_of(h, last)) for h in range(g)) + uses_of(g, last).index(what)
            return n, b * USES + n

        def step_of(b, g):
            return b * NG + g

        STACK_DMAS = 2 * 3 + 1
        order = {n: dict(src=by_head, dst=as_by_head) if n in "qk" else {} for n in "qkv"}

        def add_probs(eng, s, mt, first=False):
            eng.wait_ge(exp_done, SLOTS * s + HG * (mt + 1))
            if mt == 1:
                if not first:
                    eng.wait_ge(sums_full, s)
                so_far = probs[:, 0, :, :]
            else:
                eng.wait_ge(probs_added, (TT - 1) * s + mt - 1)
                so_far = probs_sum[:, :, :]
            eng.tensor_tensor(probs_sum[:, :, :], so_far, probs[:, mt, :, :], ALU.add
                              ).then_inc(probs_added, 1)

        block = ctx.enter_context(nc.Block())

        @block.sync
        def _(sp):
            sp.dma_start(x_sb[:, :, :], x[0].rearrange("(t p) d -> p t d", p=P)).then_inc(x_in, DMA)
            for i, src in enumerate((norm_w, norm_b)):
                sp.dma_start(small_rows[KT * i:KT * (i + 1), :], src.rearrange("(t p) -> t p", p=P)
                             ).then_inc(norm_in, DMA)

            def load_weight(n, w):
                sp.dma_start(w_raw[n], w.rearrange("(t p) n -> p t n", p=P)).then_inc(w_in[n], DMA)

            def load_emb(i, part):
                sp.dma_start(emb[i][part], films[i][part * 2 * P:(part + 1) * 2 * P, :]
                             .rearrange("(c p) n -> p c n", p=P)).then_inc(emb_in, DMA)

            load_weight("q", q_w)
            sp.dma_start(mask_full, mask).then_inc(mask_in, DMA)
            sp.dma_start(mb1_full, mask1).then_inc(mask_in, DMA)
            load_weight("k", k_w)
            sp.dma_start(cond_rows, cond).then_inc(cond_in, DMA)
            for dst, src in ((raw_bias[:, 0, :], q_b), (raw_bias[:, 1, :], k_b), (v_bias[:, :], v_b)):
                sp.dma_start(dst, src.partition_broadcast(P)).then_inc(bias_in, DMA)
            load_weight("v", v_w)
            at = 0
            for v in b_vectors:
                n = v.shape[0] // P
                sp.dma_start(b_rows[at:at + n, :], v.rearrange("(t p) -> t p", p=P)).then_inc(b_rows_in, DMA)
                at += n
            sp.wait_ge(mb_step, 6)
            sp.dma_start(mb_dram, mb).then_inc(mb_stored, DMA)
            sp.dma_start(mb1_dram, mb1_full).then_inc(mb_stored, DMA)
            sp.wait_ge(mb_stored, 2 * DMA)

            def mask_rows(b, g):
                sp.dma_start(k_stack[96:98, g, :, :].bitcast(F32),
                             mb_dram[b].unsqueeze(1).broadcast_to([2, HG, T])).then_inc(stack_in[g], DMA)

            def stack(n, g):
                parts = {"q": (0, 1, 0), "k": (0, 0, 1)}[n]
                dst = {"q": q_stack, "k": k_stack}[n]
                for row, part in enumerate(parts):
                    sp.dma_start(dst[DH0 * row:DH0 * row + DH0, g, :, :].bitcast(F32),
                                 stage[n][:, part, :].bitcast(F32)).then_inc(stack_in[g], DMA)

            def shift_rows(b, g, count):
                sp.wait_ge(work_read, count)
                for part in range(2):
                    sp.dma_start(q_stack[ROWS_MAX + part:ROWS_MAX + part + 1, g, :, :].bitcast(F32),
                                 shift[:, part, :].bitcast(F32)).then_inc(shift_in[g], DMA)

            sp.wait_ge(ones_set, 1)
            for rows in (q_stack[96:98, :, :, :], k_stack[98:100, :, :, :]):
                sp.dma_start(rows.bitcast(F32).rearrange("p g j t -> p (g j) t"),
                             ones.unsqueeze(1).broadcast_to([2, NG * HG, T])).then_inc(ones_in, DMA)
            mask_rows(0, 0)
            mask_rows(0, 1)
            sp.wait_ge(work_full, TT)
            load_emb(0, 0)
            for i in range(2):
                sp.wait_ge(w_split, i + 1)
                sp.wait_ge(bias_made, i + 1)
                load_emb(0, 1 + i)
            sp.wait_ge(cols_made, 3)
            load_emb(0, 3)
            for g in range(2):
                for i, n in enumerate("qk"):
                    sp.wait_ge(work_read, TT + 2 * g + i + 1)
                    stack(n, g)
            sp.wait_ge(film_full, 1)
            sp.wait_ge(w_split, 3)
            sp.wait_ge(bias_made, 3)
            for part in range(4):
                load_emb(1, part)
            shift_rows(0, 0, FIRST_USES.index("m") + 1)

            def step(b, g, last=False, first=False):
                if not last or g < NG - 2:
                    s_b, s_g = (b, g + 2) if g + 2 < NG else (b + 1, g + 2 - NG)
                    if not (first and g + 2 < NG):
                        sp.wait_ge(exp_full, SLOTS * (step_of(b, g) - 1))
                    mask_rows(s_b, s_g)
                if g == 2 and not last:
                    sp.wait_ge(work_full, use(b, 1, f"x{TT - 1}")[1] + 1)
                    if not (type(b) is int and b + 2 >= B):
                        load_x(b + 2)
                if not last or g < NG - 2:
                    sp.wait_ge(work_read, use(b, g, "q", last)[1] + 1)
                    stack("q", s_g)
                if not (first and g == 0):
                    store_y(b, g - 1) if g else store_y(b - 1, NG - 1)
                if not last or g < NG - 2:
                    sp.wait_ge(work_read, use(b, g, "k", last)[1] + 1)
                    stack("k", s_g)
                if g == 0 and not first:
                    store_sums(b - 1)
                if not last or g < NG - 1:
                    n_b, n_g = (b, g + 1) if g + 1 < NG else (b + 1, 0)
                    shift_rows(n_b, n_g, use(b, g, "m", last)[1] + 1)

            def load_x(b):
                sp.dma_start(x_sb[:, :, :], x[b].rearrange("(t p) d -> p t d", p=P)).then_inc(x_in, DMA)

            def store_y(b, g):
                sp.wait_ge(y_read, step_of(b, g) + 1)
                sp.dma_start(yT_dram[b].rearrange("(j g l) t -> g j l t", j=HG, g=NG)[g], y_stage[:, g % 2, :]).then_inc(y_stored[g % 2], DMA)

            def store_sums(b):
                sp.wait_ge(sums_read, b + 1)
                for j in range(HG):
                    sp.dma_start(sums_dram[b][NG * j:NG * j + NG, :], sums_stage[DH0 * j:DH0 * j + NG, :]
                                 ).then_inc(sums_stored, DMA)

            sp.wait_ge(film_full, 2)
            load_x(1)
            for g in range(NG):
                step(0, g, first=True)
            with sp.Fori(1, B - 2) as b:
                for g in range(NG):
                    step(b, g)
            for g in range(NG):
                step(B - 2, g)
            for g in range(NG):
                step(B - 1, g, last=True)
            store_y(B - 1, NG - 1)
            store_sums(B - 1)
            for i in range(2):
                sp.wait_ge(y_stored[i], DMA * B * NG // 2)
            sp.wait_ge(sums_stored, DMA * HG * B)

        @block.gpsimd
        def _(pool):
            pool.memset(minus_half[:, :], -0.5).then_inc(ident_zero, 1)
            pool.memset(ident[:, :], 0.0).then_inc(ident_zero, 1)
            pool.wait_ge(ident_zero, 2)
            pool.affine_select(out=ident[:, :], in_=ident[:, :], compare_op=ALU.not_equal, fill=1.0,
                               base=0, pattern=[[-1, P]], channel_multiplier=1).then_inc(ident_done, 1)

            def inverse_deviation(b):
                pool.wait_ge(ln_stats, 3 * (b + 1))
                if not (type(b) is int and b == 0):
                    pool.wait_ge(xhat_done, TT * b)
                pool.tensor_tensor(rstd[:, :], var_eps[:, :], minus_half[:, :], ALU.pow).then_inc(rstd_done, 1)

            def step(b, g, first=False, last=False):
                s = step_of(b, g)
                if last and g == NG - 1:
                    return
                add_probs(pool, s, 1, first)
                add_probs(pool, s, 2)
                if g == 0 and not last:
                    inverse_deviation(b + 1)
                add_probs(pool, s, 3)

            inverse_deviation(0)
            for g in range(NG):
                step(0, g, first=(g == 0))
            with pool.Fori(1, B - 1) as b:
                for g in range(NG):
                    step(b, g)
            for g in range(NG):
                step(B - 1, g, last=True)

        @block.tensor
        def _(pe):
            def three_passes(out, lhs, rhs):
                n = 0
                for kt in range(KT):
                    for a, c in ((0, 0), (0, 1), (1, 0)):
                        last = pe.matmul(out, lhs(a, kt), rhs(c, kt), start=(n == 0), stop=(n == 3 * KT - 1))
                        n += 1
                return last

            wq_parts = {n: (w_hi[n], w_lo[n]) for n in "qkv"}
            xT = (xT_hi, xT_lo)

            def take_bank(n):
                static, number = n
                if static >= 2:
                    pe.wait_ge(work_read, number - 1)
                return work_bank[static % 2][:, :]

            def project_quarter(what, g, out, kt, first, stop):
                for i, (a, c) in enumerate(((0, 0), (0, 1), (1, 0))):
                    if what in "qk":
                        lhs, rhs = wq_parts[what][a][:, kt, g * P:(g + 1) * P], xT[c][:, kt, :]
                    else:
                        lhs, rhs = xT[c][:, kt, g * P:(g + 1) * P], wq_parts["v"][a][:, kt, :]
                    last = pe.matmul(out, lhs, rhs, start=(first and i == 0), stop=(stop and i == 2))
                if stop:
                    last.then_inc(work_full, 1)

            def transpose_x(tt, number):
                out = take_bank(number)
                for kt in range(KT):
                    last = pe.transpose(out[:, kt * P:(kt + 1) * P], x_sb[:, tt, kt * P:(kt + 1) * P], ident[:, :])
                last.then_inc(work_full, 1)

            def max_scores(b, g, m, first=False):
                j, nt = m // TT, m % TT
                if m == 0:
                    pe.wait_ge(stack_in[g], DMA * STACK_DMAS * (b + 1))
                if not (first and m < 2):
                    pe.wait_ge(max_done, SLOTS * step_of(b, g) + m - 1)
                pe.matmul(max_bank[m % 2][:, :], q_stack[0:ROWS_MAX, g, j, nt * P:(nt + 1) * P],
                          k_stack[0:ROWS_MAX, g, j, :], start=True, stop=True).then_inc(max_full, 1)

            def transpose_max(b, g, number):
                out = take_bank(number)
                pe.wait_ge(max_done, SLOTS * (step_of(b, g) + 1))
                pe.transpose(out[0:SLOTS, 0:P], negmax[:, :], ident[:, :]).then_inc(work_full, 1)

            def exp_scores(b, g, k, first=False):
                mt, j = k // HG, k % HG
                if k == 0:
                    pe.wait_ge(shift_in[g], 2 * DMA * (b + 1))
                if not (first and k < 2):
                    pe.wait_ge(exp_done, SLOTS * step_of(b, g) + k - 1)
                pe.matmul(exp_bank[k % 2][:, :], k_stack[0:ROWS_EXP, g, j, mt * P:(mt + 1) * P],
                          q_stack[0:ROWS_EXP, g, j, :], start=True, stop=True).then_inc(exp_full, 1)

            def weigh_values(b, g, mt):
                s = step_of(b, g)
                pe.wait_ge(exp_done, SLOTS * s + HG * (mt + 1))
                pe.wait_ge(v_done, TT * b + mt + 1)
                if mt == 0 and not (type(s) is int and s == 0):
                    pe.wait_ge(y_read, s)
                for j in range(HG):
                    last = pe.matmul(y_bank[DH0 * j:DH0 * (j + 1), :],
                                     v_sb[:, mt, P * j + DH0 * g:P * j + DH0 * (g + 1)],
                                     probs[:, mt, j, :], start=(mt == 0), stop=(mt == TT - 1))
                last.then_inc(pv_done, 1)

            def sum_probs(b, g):
                s = step_of(b, g)
                pe.wait_ge(probs_added, (TT - 1) * (s + 1))
                if type(s) is int and s == 0:
                    pe.wait_ge(film_step, 2)
                if g == 0 and not (type(b) is int and b == 0):
                    pe.wait_ge(sums_read, b)
                for j in range(HG):
                    last = pe.matmul(sums_bank[DH0 * j:DH0 * (j + 1), :], head_sel[:, g, :],
                                     probs_sum[:, j, :], start=(g == 0), stop=(g == NG - 1))
                last.then_inc(sums_full, 1)

            def bias_product(n, out):
                pe.wait_ge(w_in[n], DMA)
                for kt in range(KT):
                    last = pe.matmul(out[:, :], nb_rep[:, kt, :], w_raw[n][:, kt, :], start=(kt == 0), stop=(kt == KT - 1))
                last.then_inc(bias_made, 1)

            def film_products(i):
                pe.wait_ge(emb_in, DMA * 4 * (i + 1))
                for half, out in enumerate((sums_bank, y_bank)):
                    for c in range(CT // HG):
                        for j in range(HG):
                            last = pe.matmul(out[DH0 * j:DH0 * (j + 1), :], condT[:, HG * c + j, :],
                                             emb[i][2 * c + j // 2][:, j % 2, half * D:(half + 1) * D], start=(c == 0), stop=(c == CT // HG - 1))
                last.then_inc(film_full, 1)

            def film_columns(i):
                pe.wait_ge(film_copied, 2 * (i + 1))
                for dt in range(TE // P):
                    last = pe.matmul((exp_bank[1], sums_bank)[i][:, dt * B:(dt + 1) * B],
                                     film_rows.rearrange("p h n -> p (h n)")[:, dt * P:(dt + 1) * P], row_sel[:, :],
                                     start=True, stop=True)
                last.then_inc(film_made, 1)

            pe.wait_ge(ident_done, 1)
            pe.wait_ge(norm_in, 2 * DMA)
            pe.transpose(max_bank[0][:, 0:2 * KT], small_rows[:, :], ident[0:2 * KT, 0:2 * KT]).then_inc(cols_made, 1)
            pe.wait_ge(mask_in, 2 * DMA)
            for i, m in enumerate((mask_full, mb1_full)):
                for tt in range(TT):
                    last = pe.transpose(max_bank[1][:, (i * TT + tt) * B:(i * TT + tt + 1) * B], m[:, tt * P:(tt + 1) * P],
                                        ident[0:B, 0:B])
            last.then_inc(cols_made, 1)
            pe.wait_ge(cond_act, 1)
            for ct in range(CT):
                last = pe.transpose(y_bank[:, ct * B:(ct + 1) * B], cond_rows[:, ct * P:(ct + 1) * P], ident[0:B, 0:B])
            last.then_inc(cond_turned, 1)
            for tt in range(TT):
                pe.wait_ge(xhat_done, tt + 1)
                transpose_x(tt, (tt, tt))

            def project(what, g, number):
                out = take_bank((number, number))
                for kt in range(KT):
                    project_quarter(what, g, out, kt, kt == 0, kt == KT - 1)

            pe.wait_ge(nb_rep_done, 1)
            for i, what in enumerate("qk"):
                bias_product(what, exp_bank[i])
                if i == 0:
                    pe.wait_ge(work_read, TT)
                pe.wait_ge(w_split, i + 1)
                project(what, 0, TT + i)
                pe.wait_ge(bias_full, i + 1)
                for g in range(NG):
                    last = pe.transpose(exp_bank[i][:, g * P:(g + 1) * P], full_bias[:, i, g * P:(g + 1) * P], ident[:, :])
                last.then_inc(bias_turned, 1)
            pe.wait_ge(cols_done, 1)
            pe.wait_ge(b_rows_in, DMA * len(b_vectors))
            pe.transpose(max_bank[0][:, 0:B_ROWS], b_rows, ident[0:B_ROWS, 0:B_ROWS]).then_inc(cols_made, 1)
            pe.wait_ge(condT_done, 1)
            project("q", 1, TT + 2)
            project("k", 1, TT + 3)
            film_products(0)
            pe.wait_ge(cols_done, 3)
            for m in range(SLOTS):
                max_scores(0, 0, m, first=True)
                if m == 2:
                    pe.wait_ge(film_copied, 2)
                    bias_product("v", y_bank)
                if m == 8:
                    pe.wait_ge(row_sel_done, 1)
                    pe.wait_ge(bias_done, 2)
                    film_columns(0)
            n = TT + 4
            transpose_max(0, 0, (n, n))
            pe.wait_ge(w_split, 3)
            project("v", 0, n + 1)
            project("v", 1, n + 2)
            pe.wait_ge(v_bias_done, 1)
            film_products(1)
            pe.wait_ge(film_step, 1)
            pe.wait_ge(ones_in, 2 * DMA)

            def exp_slot(b, g, e, first=False):
                exp_scores(b, g, e, first)
                before = (b, g - 1) if g else (b - 1, NG - 1)
                if e in (6, 10, 14):
                    weigh_values(b, g, (e - 6) // 4)
                if e == 2 and not first:
                    weigh_values(*before, TT - 1)
                if e == 7 and not first:
                    sum_probs(*before)

            def step(b, g, last=False, first=False):
                banks = {}
                has_next = not last or g < NG - 1
                n_b, n_g = (b, g + 1) if g + 1 < NG else (b + 1, 0)
                for k in range(SLOTS):
                    if not (first and g == 0 and k < LAG):
                        exp_slot(*exp_of(b, g, k), first and g == 0)
                    if first and g == 0 and k == LAG:
                        film_columns(1)
                    if has_next:
                        for m in maxima(k)[:1]:
                            max_scores(n_b, n_g, m)
                        if k == MAX_TURN:
                            transpose_max(n_b, n_g, use(b, g, "m", last))
                    for name, slots in QUARTERS.items():
                        if name in "qk":
                            if last and g >= NG - 2:
                                continue
                            what, tile, u = name, (g + 2) % NG, name
                        elif g == 0 or (g == NG - 1 and not last):
                            tile = (2 if g == 0 else 0) + (name == "v'")
                            what, u = "v", f"v{tile}"
                        else:
                            continue
                        for kt in range(KT):
                            if slots[kt] != k:
                                continue
                            if name == "q" and kt == 0 and g == 2:
                                pe.wait_ge(work_read, use(b, 1, f"x{TT - 1}")[1] + 1)
                            if kt == 0:
                                banks[name] = take_bank(use(b, g, u, last))
                            project_quarter(what, tile, banks[name], kt, kt == 0, kt == KT - 1)
                    if g == 1 and not last and k in X_TURNS:
                        tt = X_TURNS.index(k)
                        pe.wait_ge(xhat_done, TT * (b + 1) + tt + 1)
                        transpose_x(tt, use(b, 1, f"x{tt}"))
                    if has_next:
                        for m in maxima(k)[1:]:
                            max_scores(n_b, n_g, m)

            for g in range(NG):
                step(0, g, first=True)
            with pe.Fori(1, B - 1) as b:
                for g in range(NG):
                    step(b, g)
            for g in range(NG):
                step(B - 1, g, last=True)
            for e in range(SLOTS - LAG, SLOTS):
                exp_slot(B - 1, NG - 1, e)
            weigh_values(B - 1, NG - 1, TT - 1)
            sum_probs(B - 1, NG - 1)

        @block.scalar
        def _(act):
            def high_of_x(tt, number, count):
                act.wait_ge(work_full, number + 1)
                act.activation(xT_hi[:, :, tt * P:(tt + 1) * P],
                               work_bank[count % 2][:, :].rearrange("p (k t) -> p k t", k=KT),
                               ACT.Copy).then_inc(hi_done, 1)

            def high_of(what, g, number, count):
                act.wait_ge(work_full, number + 1)
                act.activation(stage[what][:, 0, :], work_bank[count % 2][:, :], ACT.Identity,
                               bias=bias[what][:, g:g + 1]).then_inc(hi_done, 1)

            def mask_value(b, mt, number):
                act.wait_ge(work_read, number + 1)
                act.activation(v_sb[:, mt, :], v_sb[:, mt, :], ACT.Copy, scale=mask_scale(b, mt)
                               ).then_inc(v_done, 1)

            def mask_scale(b, mt):
                return mask_col[:, mt, bass.ds(b, 1)]

            def exp(b, g, k, first=False):
                mt, j = k // HG, k % HG
                s = step_of(b, g)
                act.wait_ge(exp_full, SLOTS * s + k + 1)
                if j == 0 and not first:
                    act.wait_ge(pv_done, TT * (s - 1) + mt + 1)
                    act.wait_ge(probs_added, (TT - 1) * (s - 1) + max(mt, 1))
                act.activation(probs[:, mt, j, :], exp_bank[k % 2][:, :], ACT.Exp).then_inc(exp_done, 1)

            def copy_y(b, g):
                s = step_of(b, g)
                act.wait_ge(pv_done, TT * (s + 1))
                if not (type(b) is int and b == 0 and g < 2):
                    act.wait_ge(y_stored[g % 2], DMA * (b * (NG // 2) + g // 2))
                act.activation(y_stage[:, g % 2, :], y_bank[:, :], ACT.Copy).then_inc(y_read, 1)

            def copy_sums(b):
                act.wait_ge(sums_full, NG * (b + 1))
                if not (type(b) is int and b == 0):
                    act.wait_ge(sums_stored, DMA * HG * b)
                act.activation(sums_stage[:, :], sums_bank[:, :], ACT.Copy).then_inc(sums_read, 1)

            def high_of_w(n):
                act.wait_ge(w_in[n], DMA)
                high_of_weight(act, w_raw[n], nw, w_hi[n], w_hi_done[n], **order[n])

            def copy_film(i):
                act.wait_ge(film_full, i + 1)
                for half, src in enumerate((sums_bank, y_bank)):
                    act.activation(film_rows[:, half, :], src[:, :], ACT.Copy).then_inc(film_copied, 1)

            act.wait_ge(cond_in, DMA)
            act.activation(cond_rows, cond_rows, ACT.Silu).then_inc(cond_act, 1)
            act.wait_ge(cols_done, 1)
            high_of_w("q")
            for tt in range(TT):
                high_of_x(tt, tt, tt)
            high_of_w("k")
            act.wait_ge(bias_done, 2)
            n = TT
            for g in range(2):
                for what in "qk":
                    if g == 1:
                        act.wait_ge(stack_in[0], DMA * STACK_DMAS)
                    high_of(what, g, n, n)
                    n += 1
            copy_film(0)
            high_of_w("v")
            act.wait_ge(cols_done, 2)
            mask_value(0, 0, n + 1)
            mask_value(0, 1, n + 2)
            copy_film(1)

            def exp_slot(b, g, e, first=False):
                exp(b, g, e, first)
                if e == 2 and not first:
                    copy_y(*((b, g - 1) if g else (b - 1, NG - 1)))
                if e == 8 and g == 0 and not first:
                    copy_sums(b - 1)

            def step(b, g, last=False, first=False):
                for k in range(SLOTS):
                    if not (first and g == 0 and k < LAG):
                        exp_slot(*exp_of(b, g, k), first and g == 0)
                    for what in "qk":
                        if k == QUARTERS[what][-1] and (not last or g < NG - 2):
                            p_b, p_g = (b, g + 1) if g + 1 < NG else (b + 1, 0)
                            act.wait_ge(stack_in[p_g], DMA * STACK_DMAS * (p_b + 1))
                            static, number = use(b, g, what, last)
                            high_of(what, (g + 2) % NG, number, static)
                    if g == 1 and not last and k in X_TURNS:
                        tt = X_TURNS.index(k)
                        static, number = use(b, 1, f"x{tt}")
                        high_of_x(tt, number, static)
                    if k == 12 and (g == 0 or (g == NG - 1 and not last)):
                        mt = 2 if g == 0 else 0
                        mask_value(b if g == 0 else b + 1, mt, use(b, g, f"v{mt}", last)[1])
                if g == 0 or (g == NG - 1 and not last):
                    mt = 3 if g == 0 else 1
                    mask_value(b if g == 0 else b + 1, mt, use(b, g, f"v{mt}", last)[1])

            for g in range(NG):
                step(0, g, first=True)
            with act.Fori(1, B - 1) as b:
                for g in range(NG):
                    step(b, g)
            for g in range(NG):
                step(B - 1, g, last=True)
            for e in range(SLOTS - LAG, SLOTS):
                exp_slot(B - 1, NG - 1, e)
            copy_y(B - 1, NG - 1)
            copy_sums(B - 1)

        @block.vector
        def _(dve):
            def statistics_of_x(b):
                dve.wait_ge(x_in, DMA * (b + 1))
                for tt in range(TT):
                    last = dve.bn_stats(stats[:, tt, :], x_sb[:, tt, :])
                last.then_inc(ln_stats, 1)
                dve.wait_ge(ln_stats, 3 * b + 1)
                dve.memset(var_eps[:, :], EPS)
                for tt in range(TT):
                    last = dve.bn_aggr(mv[:, tt, :], stats[:, tt, :])
                last.then_inc(ln_stats, 1)
                dve.wait_ge(ln_stats, 3 * b + 2)
                dve.tensor_tensor(var_eps[:, :], mv[:, :, 1], var_eps[:, :], ALU.add).then_inc(ln_stats, 1)

            def normalise_x(b, tiles):
                dve.wait_ge(rstd_done, b + 1)
                for tt in tiles:
                    dve.tensor_scalar(x_sb[:, tt, :], x_sb[:, tt, :], mv[:, tt, 0:1], rstd[:, tt:tt + 1],
                                      ALU.subtract, ALU.mult).then_inc(xhat_done, 1)

            def low_of_x(tt, static, hi_count):
                dve.wait_ge(hi_done, hi_count)
                cols = slice(tt * P, (tt + 1) * P)
                dve.tensor_tensor(xT_lo[:, :, cols], work_bank[static % 2][:, :].rearrange("p (k t) -> p k t", k=KT),
                                  xT_hi[:, :, cols].bitcast(F32), ALU.subtract).then_inc(work_read, 1)

            def low_of(what, g, static, hi_count):
                dve.wait_ge(hi_done, hi_count)
                dve.scalar_tensor_tensor(out=stage[what][:, 1, :], in0=work_bank[static % 2][:, :],
                                         scalar=bias[what][:, g:g + 1], in1=stage[what][:, 0, :].bitcast(F32),
                                         op0=ALU.add, op1=ALU.subtract).then_inc(work_read, 1)

            def add_value_bias(b, mt, static, number):
                dve.wait_ge(work_full, number + 1)
                if not (type(b) is int and b == 0):
                    dve.wait_ge(pv_done, TT * (step_of(b, 0) - 1) + mt + 1)
                dve.tensor_tensor(v_sb[:, mt, :], work_bank[static % 2][:, :], v_bias[:, :], ALU.add
                                  ).then_inc(work_read, 1)

            def maximum(b, g, m):
                dve.wait_ge(max_full, SLOTS * step_of(b, g) + m + 1)
                dve.tensor_reduce(negmax[:, m:m + 1], max_bank[m % 2][:, :], AXX, ALU.max, negate=True
                                  ).then_inc(max_done, 1)

            def split_shift(b, g, static, number):
                s = step_of(b, g)
                dve.wait_ge(work_full, number + 1)
                if not (type(s) is int and s == 0):
                    p_b, p_g = (b, g - 1) if g else (b - 1, NG - 1)
                    dve.wait_ge(shift_in[p_g], 2 * DMA * (p_b + 1))
                dve.tensor_copy(shift[:, 0, :], work_bank[static % 2][0:SLOTS, 0:P]).then_inc(shift_hi, 1)
                dve.wait_ge(shift_hi, s + 1)
                dve.tensor_tensor(shift[:, 1, :], work_bank[static % 2][0:SLOTS, 0:P],
                                  shift[:, 0, :].bitcast(F32), ALU.subtract).then_inc(work_read, 1)

            dve.memset(ones, 1.0).then_inc(ones_set, 1)
            dve.memset(head_sel[:, :, :], 0.0).then_inc(head_sel_zero, 1)
            dve.wait_ge(head_sel_zero, 1)
            for g in range(NG):
                last = dve.memset(head_sel[:, g, g:g + 1], 1.0)
            dve.memset(condT[:, :, :], 0.0)
            statistics_of_x(0)
            dve.wait_ge(cols_made, 1)
            dve.tensor_copy(small_cols[:, :], max_bank[0][:, 0:2 * KT]).then_inc(cols_done, 1)
            dve.wait_ge(cols_done, 1)
            dve.tensor_copy(nb_rep, nb.unsqueeze(2).broadcast_to([P, KT, P])).then_inc(nb_rep_done, 1)
            normalise_x(0, range(TT))
            dve.wait_ge(cols_made, 2)
            for i, m in enumerate((mask_col, shared.mask1_col)):
                last = dve.tensor_copy(m[:, :, :], max_bank[1][:, i * TT * B:(i + 1) * TT * B]
                                       .rearrange("p (t b) -> p t b", t=TT))
            last.then_inc(cols_done, 1)
            dve.tensor_scalar(mb_full, mask_full, -1.0, 1.0, ALU.mult, ALU.add).then_inc(mb_step, 1)
            dve.tensor_scalar(mb1_full, mb1_full, -1.0, 1.0, ALU.mult, ALU.add).then_inc(mb_step, 1)
            dve.wait_ge(mb_step, 2)
            dve.tensor_scalar(mb_full, mb_full, -BIG, None, ALU.mult).then_inc(mb_step, 1)
            dve.tensor_scalar(mb1_full, mb1_full, -BIG, None, ALU.mult).then_inc(mb_step, 1)
            dve.wait_ge(mb_step, 3)
            dve.tensor_copy(mb[:, 0, :].bitcast(F32R), mb_full).then_inc(mb_step, 1)
            dve.wait_ge(mb_step, 5)
            dve.tensor_tensor(mb[:, 1, :].bitcast(F32R), mb_full, mb[:, 0, :], ALU.subtract).then_inc(mb_step, 1)

            def low_of_w(n):
                low_of_weight(dve, w_raw[n], nw, w_hi[n], w_lo[n], w_hi_done[n], w_split, **order[n])

            low_of_w("q")
            for tt in range(TT):
                low_of_x(tt, tt, tt + 1)
            dve.wait_ge(bias_in, 3 * DMA)

            def add_bias(i):
                dve.wait_ge(bias_made, i + 1)
                dve.tensor_tensor(as_by_head(full_bias[:, i, :]), by_head(exp_bank[i][:, :]), by_head(raw_bias[:, i, :]),
                                  ALU.add).then_inc(bias_full, 1)

            def copy_bias(i):
                dve.wait_ge(bias_turned, i + 1)
                dve.tensor_copy(bias_cols[:, i, :], exp_bank[i][:, :].rearrange("p (g c) -> p g c", g=NG)[:, :, 0]
                                ).then_inc(bias_done, 1)

            add_bias(0)
            dve.wait_ge(cond_turned, 1)
            dve.tensor_copy(condT[:, :, 0:B], y_bank[:, 0:CT * B].rearrange("p (c b) -> p c b", c=CT)
                            ).then_inc(condT_done, 1)
            dve.tensor_reduce(row_sel[:, :], ident[:, :].rearrange("p (j b) -> p b j", j=HG)[:, 0:B, :], AXX, ALU.add
                              ).then_inc(row_sel_done, 1)
            low_of_w("k")
            copy_bias(0)
            add_bias(1)
            copy_bias(1)
            dve.wait_ge(bias_done, 2)
            n = TT
            for what in "qk":
                low_of(what, 0, n, n + 1)
                n += 1
            dve.wait_ge(cols_made, 3)
            dve.tensor_copy(shared.cols[:, :], max_bank[0][:, 0:B_ROWS]).then_inc(cols_done, 1)

            def by_row(column):
                return column.unsqueeze(2).broadcast_to([P, KT, B])

            film_a, film_b = shared.film_a, shared.film_b

            def add_film_bias(i):
                dve.wait_ge(film_made, i + 1)
                e = (exp_bank[1], sums_bank)[i][:, 0:2 * KT * B].rearrange("p (c b) -> p c b", b=B)
                dve.tensor_tensor(film_a[i][:, :, :], e[:, 0:KT, :], by_row(shared.eb[i][:, 0:KT]), ALU.add)
                dve.tensor_tensor(film_b[i][:, :, :], e[:, KT:2 * KT, :], by_row(shared.eb[i][:, KT:2 * KT]), ALU.add
                                  ).then_inc(film_step, 1)

            for what in "qk":
                low_of(what, 1, n, n + 1)
                n += 1
            n -= 1
            for m in range(SLOTS):
                maximum(0, 0, m)
                if m == 6:
                    low_of_w("v")
                if m == 10:
                    dve.wait_ge(bias_made, 3)
                    dve.tensor_tensor(v_bias[:, :], y_bank[:, :], v_bias[:, :], ALU.add).then_inc(v_bias_done, 1)
            dve.wait_ge(cols_done, 3)
            add_film_bias(0)
            split_shift(0, 0, n + 1, n + 1)
            dve.wait_ge(v_bias_done, 1)
            add_value_bias(0, 0, n + 2, n + 2)
            add_value_bias(0, 1, n + 3, n + 3)
            def finish_film():
                add_film_bias(1)
                dve.wait_ge(film_step, 2)
                for i in range(2):
                    dve.tensor_scalar(film_a[i][:, :, :], film_a[i][:, :, :], 1.0, None, ALU.add).then_inc(film_step, 1)
                dve.wait_ge(film_step, 4)
                for i in range(2):
                    dve.tensor_tensor(film_c[:, i, :, :], film_a[i][:, :, :], by_row(shared.n2b[i]), ALU.mult
                                      ).then_inc(film_step, 1)
                dve.wait_ge(film_step, 6)
                for i in range(2):
                    dve.tensor_tensor(film_a[i][:, :, :], film_a[i][:, :, :], by_row(shared.n2w[i]), ALU.mult)
                    dve.tensor_tensor(film_b[i][:, :, :], film_b[i][:, :, :], film_c[:, i, :, :], ALU.add)

            HIGHS = 2 * NG + TT

            def high_count(b, g, i):
                return TT + 4 + HIGHS * b + (2 * g + (TT if g > 1 else 0)) + i + 1

            def step(b, g, last=False):
                has_next = not last or g < NG - 1
                n_b, n_g = (b, g + 1) if g + 1 < NG else (b + 1, 0)
                for k in range(SLOTS):
                    if has_next:
                        for m in maxima(k):
                            maximum(n_b, n_g, m)
                    for i, what in enumerate("qk"):
                        if k == QUARTERS[what][-1] + 1 and (not last or g < NG - 2):
                            low_of(what, (g + 2) % NG, use(b, g, what, last)[0], high_count(b, g, i))
                    if g == 1 and not last and 3 <= k < 3 + TT:
                        normalise_x(b + 1, [k - 3])
                    if g == 1 and not last and k - 1 in X_TURNS:
                        tt = X_TURNS.index(k - 1)
                        low_of_x(tt, use(b, 1, f"x{tt}")[0], high_count(b, 1, 2 + tt))
                    if k == 11 and (g == 0 or (g == NG - 1 and not last)):
                        mt = 2 if g == 0 else 0
                        add_value_bias(b if g == 0 else b + 1, mt, *use(b, g, f"v{mt}", last))
                    if has_next and k == MAX_TURN:
                        split_shift(n_b, n_g, *use(b, g, "m", last))
                    if g == 0 and not last and k == 13:
                        statistics_of_x(b + 1)
                        if type(b) is int and b == 0:
                            finish_film()
                if g == 0 or (g == NG - 1 and not last):
                    mt = 3 if g == 0 else 1
                    add_value_bias(b if g == 0 else b + 1, mt, *use(b, g, f"v{mt}", last))

            for g in range(NG):
                step(0, g)
            with dve.Fori(1, B - 1) as b:
                for g in range(NG):
                    step(b, g)
            for g in range(NG):
                step(B - 1, g, last=True)
            for mt in range(1, TT):
                add_probs(dve, step_of(B - 1, NG - 1), mt)


def projection_phase(nc, shared, x, out0_w, out0_b, q_w, q_b, k_w, v_w, v_b, out1_w, out1_b, yT_dram, sums_dram,
                     mb_dram, out):
    B = x.shape[0]
    SILUS = KT - 1
    with ExitStack() as ctx:
        def sb(name, shape, dt=F32):
            return ctx.enter_context(nc.sbuf_tensor(name, shape, dt))

        def sem(name):
            return ctx.enter_context(nc.semaphore(name))

        WEIGHTS = ("out0", "q", "k", "v", "out1")
        w_hi = {n: sb(f"b_w{n}_hi", [P, KT, D], F32R) for n in WEIGHTS}
        w_lo = {n: sb(f"b_w{n}_lo", [P, KT, D], F32R) for n in WEIGHTS}
        area0 = sb("area0", [P, 4, TT * D])
        area1 = sb("area1", [P, 4, TT * D])

        def tiles(area, i):
            return area[:, i, :].rearrange("p (t n) -> p t n", t=TT)

        yT_sb, x_sb, yn, x1hat = (tiles(area0, i) for i in range(4))
        ekT, ek, v_sb, q_sb = (tiles(area1, i) for i in range(4))
        eqT = ekT
        w_raw = {n: tiles(area1, i) for i, n in enumerate(("k", "out1", "v", "q"))}
        result = sb("result", [P, TT, D])
        w_raw["out0"] = result[:, :, :]
        silu = sb("silu", [P, SILUS, T])
        sT_hi = sb("sT_hi", [P, KT, T], F32R)
        sT_lo = sb("sT_lo", [P, KT, T], F32R)
        x1T_hi = sb("x1T_hi", [P, KT, T], F32R)
        x1T_lo = sb("x1T_lo", [P, KT, T], F32R)
        sums_sb = sb("b_sums", [H0, T])
        mask_bias = sb("mask_bias", [P, T])
        rows = {n: sb(f"row_{n}", [P, D]) for n in ("out0", "q", "v", "out1")}
        att_bd = sb("att_bd", [P, KT, P])
        lnb_rep = att_bd
        ident, film_a, film_b, mask_col = shared.ident, shared.film_a, shared.film_b, shared.mask1_col
        k_bias = sb("b_k_bias", [P, NG])
        stats = sb("b_stats", [P, TT, 6])
        mv = {n: sb(f"mv_{n}", [P, TT, 2]) for n in ("y0", "x1", "y1")}
        var_eps = {n: sb(f"var_eps_{n}", [P, TT]) for n in ("y0", "x1", "y1")}
        rstd = {n: sb(f"rstd_{n}", [P, TT]) for n in ("y0", "x1", "y1")}
        minus_half = sb("b_minus_half", [P, TT])
        rinv0 = sb("rinv0", [P, TT, H0])
        kmax = sb("kmax", [P, NG])
        ksum = sb("ksum", [P, NG])
        krec = sb("krec", [P, NG])
        qmax, qsum = rinv0[:, :, 0:H1], rinv0[:, :, H1:2 * H1]
        qrec = qsum

        RING = 6
        work_bank = [ctx.enter_context(nc.psum_tensor(f"b_work{i}", [P, 512], F32)) for i in range(RING)]
        sums_bank = ctx.enter_context(nc.psum_tensor("b_sums_bank", [P, 512], F32))
        att_bank = ctx.enter_context(nc.psum_tensor("b_att_bank", [P, 512], F32))

        rows_in = sem("rows_in")
        w_in = {n: sem(f"b_w{n}_in") for n in WEIGHTS}
        lnb_rep_done = sem("lnb_rep_done")
        bias_made, bias_done = sem("b_bias_made"), sem("b_bias_done")
        w_hi_done, w_split = {n: sem(f"b_w{n}_hi_done") for n in WEIGHTS}, sem("b_w_split")
        const_set = sem("b_const_set")
        y_in, mask_bias_in = sem("y_in"), sem("mask_bias_in")
        x_in, stored = ([sem(f"{n}{tt}") for tt in range(TT)] for n in ("b_x_in", "b_stored"))
        work_full, bank_read = sem("b_work_full"), [sem(f"bank_read{i}") for i in range(RING)]
        sums_turned, rinv0_done = sem("sums_turned"), sem("rinv0_done")
        ln_step = {n: sem(f"ln_step_{n}") for n in ("y0", "x1", "y1")}
        rstd_done = {n: sem(f"rstd_done_{n}") for n in ("y0", "x1", "y1")}
        hat_done = {n: sem(f"hat_done_{n}") for n in ("y0", "x1", "y1")}
        sT_hi_done, sT_lo_done, x1T_hi_done = sem("sT_hi_done"), sem("sT_lo_done"), sem("x1T_hi_done")
        x_biased, result_biased = sem("x_biased"), sem("result_biased")
        k_max_done, k_exp_done, krec_done = sem("k_max_done"), sem("k_exp_done"), sem("krec_done")
        q_max_done, q_shifted, q_exp_done = sem("q_max_done"), sem("q_shifted"), sem("q_exp_done")
        q_sum_done, qrec_done, v_done = sem("q_sum_done"), sem("qrec_done"), sem("b_v_done")
        att_made, att_done = sem("att_made"), sem("att_done")

        def tiles_of(letters):
            return [(c, tile) for c in letters for tile in range(TILES)]

        TILES = 4
        ORDER = tiles_of("KLAVMSH") + [("Q", 0), ("Q", 1)] + tiles_of("C") + [("Q", 2), ("Q", 3)] + tiles_of("XJY")
        FIRST = "ASCX"

        def order_of(kind):
            return [u for u in ORDER if not (kind == "first" and u[0] in "LM" or kind == "last" and u[0] in FIRST)]

        PER_ROW = len(ORDER)
        assert PER_ROW % RING == 0

        def use(kind, b, what, tile):
            if kind == "start":
                n = TILES * FIRST.index(what) + tile
                return n, n
            if kind == "end":
                n = len(order_of("last")) + TILES * "LM".index(what) + tile
            else:
                n = order_of(kind).index((what, tile))
            n += TILES * len(FIRST) - (0 if kind == "first" else TILES * 2)
            return n, PER_ROW * b + n


        def bank(u):
            return work_bank[u[0] % RING][:, :]

        def reads(b, u):
            return (PER_ROW // RING) * b + u[0] // RING

        def wait_read(eng, kind, b, what, tile):
            u = use(kind, b, what, tile)
            eng.wait_ge(bank_read[u[0] % RING], reads(b, u) + 1)

        def wait_x1T(eng, kind, b):
            for kt in range(KT):
                if kind == "first":
                    wait_read(eng, "start", 0, "X", kt)
                else:
                    wait_read(eng, "mid", b - 1, "X", kt)

        def film_columns(film, kt, b):
            return film[:, kt, bass.ds(b, 1)]

        block = ctx.enter_context(nc.Block())

        @block.sync
        def _(sp):
            def load_y(b):
                sp.dma_start(yT_sb, yT_dram[b].rearrange("(g p) t -> p g t", p=P)).then_inc(y_in, DMA)
                sp.dma_start(sums_sb[:, :], sums_dram[b]).then_inc(y_in, DMA)

            def load_x(b, tt):
                sp.dma_start(x_sb[:, tt, :], x[b][tt * P:(tt + 1) * P, :]).then_inc(x_in[tt], DMA)

            def load_mask_bias(b):
                sp.dma_start(mask_bias[:, :], mb_dram[b].partition_broadcast(P)).then_inc(mask_bias_in, DMA)

            def load_weight(n, w):
                sp.dma_start(w_raw[n], w.rearrange("(t p) n -> p t n", p=P)).then_inc(w_in[n], DMA)

            load_y(0)
            load_weight("out0", out0_w)
            load_weight("k", k_w)
            for tt in range(TT):
                load_x(0, tt)
            for n, v in (("out0", out0_b), ("q", q_b), ("v", v_b), ("out1", out1_b)):
                sp.dma_start(rows[n][:, :], v.partition_broadcast(P)).then_inc(rows_in, DMA)
            load_mask_bias(0)
            load_weight("v", v_w)
            load_weight("q", q_w)
            load_weight("out1", out1_w)
            sp.wait_ge(work_full, use("start", 0, "A", TT - 1)[1] + 1)
            load_y(1)

            def iteration(kind, b, more=True):
                if kind != "last":
                    for g in range(NG):
                        wait_read(sp, kind, b, "K", g)
                    load_mask_bias(b + 1)
                    if more:
                        sp.wait_ge(work_full, use(kind, b, "A", TT - 1)[1] + 1)
                        load_y(b + 2)
                for tt in range(TT + 1):
                    if kind != "first" and tt < TT:
                        store(kind, b, b - 1, tt)
                    if kind != "last" and tt:
                        sp.wait_ge(hat_done["x1"], TT * b + tt)
                        sp.wait_ge(result_biased, TT * b + tt)
                        load_x(b + 1, tt - 1)

            def store(kind, b, row, tt):
                wait_read(sp, kind, b, "M", tt)
                sp.dma_start(out[row][tt * P:(tt + 1) * P, :], result[:, tt, :]).then_inc(stored[tt], DMA)

            iteration("first", 0)
            with sp.Fori(1, B - 2) as b:
                iteration("mid", b)
            iteration("mid", B - 2, more=False)
            iteration("last", B - 1)
            for tt in range(TT):
                store("end", B - 1, B - 1, tt)
            for tt in range(TT):
                sp.wait_ge(stored[tt], DMA * B)

        @block.tensor
        def _(pe):
            def take(kind, b, what, tile):
                u = use(kind, b, what, tile)
                if u[0] >= RING:
                    pe.wait_ge(bank_read[u[0] % RING], reads(b, u))
                return bank(u)

            def three_passes(out, lhs, rhs):
                for kt in range(KT):
                    for a, c in ((0, 0), (0, 1), (1, 0)):
                        last = pe.matmul(out, lhs(a, kt), rhs(c, kt), start=(kt == 0 and a + c == 0),
                                         stop=(kt == KT - 1 and a == 1))
                last.then_inc(work_full, 1)

            def weights(n):
                return w_hi[n], w_lo[n]

            x1T, sT = (x1T_hi, x1T_lo), (sT_hi, sT_lo)

            def by_position(kind, b, what, tile, actT, w):
                out = take(kind, b, what, tile)
                three_passes(out, lambda a, kt: actT[a][:, kt, tile * P:(tile + 1) * P],
                             lambda c, kt: w[c][:, kt, :])

            def by_feature(kind, b, what, tile, w, actT):
                out = take(kind, b, what, tile)
                three_passes(out, lambda a, kt: w[a][:, kt, tile * P:(tile + 1) * P],
                             lambda c, kt: actT[c][:, kt, :])

            def turn(kind, b, what, tile, src):
                out = take(kind, b, what, tile)
                for i in range(4):
                    last = pe.transpose(out[:, i * P:(i + 1) * P], src(i), ident[:, :])
                last.then_inc(work_full, 1)

            def A(kind, b, row):
                pe.wait_ge(y_in, 2 * DMA * (row + 1))
                if not (type(row) is int and row == 0):
                    pe.wait_ge(rinv0_done, row)
                for tt in range(TT):
                    turn(kind, b, "A", tt, lambda i: yT_sb[:, i, tt * P:(tt + 1) * P])
                    if tt == 0:
                        for nt in range(TT):
                            last = pe.transpose(sums_bank[:, nt * H0:(nt + 1) * H0], sums_sb[:, nt * P:(nt + 1) * P],
                                                ident[0:H0, 0:H0])
                        last.then_inc(sums_turned, 1)

            def S(kind, b, row):
                pe.wait_ge(hat_done["y0"], TT * (row + 1))
                for kt in range(KT):
                    turn(kind, b, "S", kt, lambda i: yn[:, i, kt * P:(kt + 1) * P])

            def C(kind, b, count):
                pe.wait_ge(sT_lo_done, count)
                for tt in range(TT):
                    by_position(kind, b, "C", tt, sT, weights("out0"))

            def X(kind, b, row):
                pe.wait_ge(hat_done["x1"], TT * (row + 1))
                for kt in range(KT):
                    turn(kind, b, "X", kt, lambda i: x1hat[:, i, kt * P:(kt + 1) * P])

            def K(kind, b):
                wait_x1T(pe, kind, b)
                for g in range(NG):
                    by_feature(kind, b, "K", g, weights("k"), x1T)

            def V(kind, b):
                for tt in range(TT):
                    by_position(kind, b, "V", tt, x1T, weights("v"))

            def H(kind, b):
                pe.wait_ge(k_exp_done, NG * (b + 1))
                for tt in range(TT):
                    turn(kind, b, "H", tt, lambda i: ekT[:, i, tt * P:(tt + 1) * P])

            def Q(kind, b, tiles):
                for tt in tiles:
                    by_position(kind, b, "Q", tt, x1T, weights("q"))

            def attention(kind, b):
                for tt in range(TT):
                    wait_read(pe, kind, b, "H", tt)
                pe.wait_ge(v_done, TT * (b + 1))
                if not (type(b) is int and b == 0):
                    pe.wait_ge(att_done, b)
                for p in range(KT):
                    for tt in range(TT):
                        last = pe.matmul(att_bank[:, p * P:(p + 1) * P], ek[:, tt, p * P:(p + 1) * P],
                                         v_sb[:, tt, p * P:(p + 1) * P], start=(tt == 0), stop=(tt == TT - 1))
                last.then_inc(att_made, 1)

            def J(kind, b):
                pe.wait_ge(q_exp_done, TT * (b + 1))
                for p in range(KT):
                    turn(kind, b, "J", p, lambda i: q_sb[:, i, p * P:(p + 1) * P])

            def Y(kind, b):
                for p in range(KT):
                    wait_read(pe, kind, b, "J", p)
                pe.wait_ge(att_done, b + 1)
                for tt in range(TT):
                    out = take(kind, b, "Y", tt)
                    for p in range(KT):
                        last = pe.matmul(out[:, p * P:(p + 1) * P], eqT[:, p, tt * P:(tt + 1) * P],
                                         att_bd[:, p, :], start=True, stop=True)
                    last.then_inc(work_full, 1)

            def L(kind, b, row):
                pe.wait_ge(hat_done["y1"], TT * (row + 1))
                for kt in range(KT):
                    turn(kind, b, "L", kt, lambda i: yn[:, i, kt * P:(kt + 1) * P])

            def M(kind, b, count):
                pe.wait_ge(sT_lo_done, count)
                for tt in range(TT):
                    by_position(kind, b, "M", tt, sT, weights("out1"))

            def bias_product(n, out):
                pe.wait_ge(w_in[n], DMA)
                for kt in range(KT):
                    last = pe.matmul(out[:, :], lnb_rep[:, kt, :], w_raw[n][:, kt, :], start=(kt == 0), stop=(kt == KT - 1))
                last.then_inc(bias_made, 1)

            A("start", 0, 0)
            pe.wait_ge(rinv0_done, 1)
            pe.wait_ge(w_in["k"], DMA)
            for g in range(NG):
                for kt in range(KT):
                    last = pe.matmul(sums_bank[:, g:g + 1], w_raw["k"][:, kt, g * P:(g + 1) * P], shared.lnb[:, kt:kt + 1],
                                     start=(kt == 0), stop=(kt == KT - 1))
            last.then_inc(bias_made, 1)
            S("start", 0, 0)
            pe.wait_ge(w_split, 1)
            C("start", 0, KT)
            pe.wait_ge(lnb_rep_done, 1)
            bias_product("v", att_bank)
            pe.wait_ge(bias_done, 1)
            bias_product("q", sums_bank)
            X("start", 0, 0)
            pe.wait_ge(bias_done, 3)
            pe.wait_ge(w_split, len(WEIGHTS))

            def iteration(kind, b):
                K(kind, b)
                if kind != "first":
                    L(kind, b, b - 1)
                if kind != "last":
                    A(kind, b, b + 1)
                V(kind, b)
                if kind != "first":
                    M(kind, b, KT * (2 * b + 1))
                if kind != "last":
                    S(kind, b, b + 1)
                H(kind, b)
                Q(kind, b, (0, 1))
                if kind != "last":
                    C(kind, b, KT * (2 * b + 2))
                Q(kind, b, (2, 3))
                attention(kind, b)
                if kind != "last":
                    X(kind, b, b + 1)
                J(kind, b)
                Y(kind, b)

            iteration("first", 0)
            with pe.Fori(1, B - 1) as b:
                iteration("mid", b)
            iteration("last", B - 1)
            L("end", B - 1, B - 1)
            M("end", B - 1, KT * 2 * B)

        @block.scalar
        def _(act):
            def silus(kind, b, what, film, row, count, tiles=range(KT)):
                for kt in tiles:
                    u = use(kind, b, what, kt)
                    act.wait_ge(work_full, u[1] + 1)
                    if kt == 0 and kind != "start":
                        act.wait_ge(sT_lo_done, count)
                    if kt == KT - 1:
                        act.wait_ge(sT_lo_done, count + 1)
                    act.activation(silu[:, kt % SILUS, :], bank(u), ACT.Silu, scale=film_columns(film_a[film], kt, row),
                                   bias=film_columns(film_b[film], kt, row)).then_inc(bank_read[u[0] % RING], 1)

            def copies(kind, b, what, dst, last_reader):
                for i in range(4):
                    u = use(kind, b, what, i)
                    act.wait_ge(work_full, u[1] + 1)
                    act.activation(dst(i), bank(u), ACT.Copy
                                   ).then_inc(bank_read[u[0] % RING] if last_reader else x1T_hi_done, 1)

            def high_of_w(n):
                act.wait_ge(w_in[n], DMA)
                high_of_weight(act, w_raw[n], None if n in ("out0", "out1") else shared.lnw, w_hi[n], w_hi_done[n])

            high_of_w("out0")
            high_of_w("k")
            silus("start", 0, "S", 0, 0, 0)
            for n in ("v", "q", "out1"):
                high_of_w(n)
            copies("start", 0, "X", lambda i: x1T_hi[:, i, :], False)

            def iteration(kind, b):
                for g in range(NG):
                    if g == NG - 1 and kind != "first":
                        silus(kind, b, "L", 1, b - 1, KT * 2 * b, range(0, 2))
                    act.wait_ge(k_max_done, NG * b + g + 1)
                    act.activation(ekT[:, g, :], ekT[:, g, :], ACT.Exp, bias=kmax[:, g:g + 1],
                                   accum_out=ksum[:, g:g + 1]).then_inc(k_exp_done, 1)
                if kind != "first":
                    silus(kind, b, "L", 1, b - 1, KT * 2 * b, range(2, KT))
                for tt in range(TT):
                    wait_read(act, kind, b, "V", tt)
                    act.activation(v_sb[:, tt, :], v_sb[:, tt, :], ACT.Copy, scale=mask_col[:, tt, bass.ds(b, 1)]
                                   ).then_inc(v_done, 1)
                if kind != "last":
                    silus(kind, b, "S", 0, b + 1, KT * (2 * b + 1))
                copies(kind, b, "H", lambda i: ek[:, i, :], True)
                for tt in range(TT):
                    act.wait_ge(q_shifted, TT * b + tt + 1)
                    act.activation(q_sb[:, tt, :], q_sb[:, tt, :], ACT.Exp).then_inc(q_exp_done, 1)
                if kind != "last":
                    copies(kind, b, "X", lambda i: x1T_hi[:, i, :], False)
                copies(kind, b, "J", lambda i: eqT[:, i, :], True)

            iteration("first", 0)
            with act.Fori(1, B - 1) as b:
                iteration("mid", b)
            iteration("last", B - 1)
            silus("end", B - 1, "L", 1, B - 1, KT * (2 * B - 1))

        @block.gpsimd
        def _(pool):
            def inverse_deviation(n, row):
                pool.wait_ge(ln_step[n], 3 * (row + 1))
                pool.tensor_tensor(rstd[n][:, :], var_eps[n][:, :], minus_half[:, :], ALU.pow).then_inc(rstd_done[n], 1)

            def low_of_silu(count):
                for kt in range(KT):
                    pool.wait_ge(sT_hi_done, count + kt + 1)
                    pool.tensor_tensor(sT_lo[:, kt, :], silu[:, kt % SILUS, :], sT_hi[:, kt, :].bitcast(F32), ALU.subtract
                                       ).then_inc(sT_lo_done, 1)

            def bias_x(row):
                for tt in range(TT):
                    pool.wait_ge(x_in[tt], DMA * (row + 1))
                    pool.tensor_tensor(x_sb[:, tt, :], x_sb[:, tt, :], rows["out0"][:, :], ALU.add).then_inc(x_biased, 1)

            def bias_result(row, tiles):
                for tt in tiles:
                    pool.wait_ge(hat_done["x1"], TT * row + tt + 1)
                    if not (type(row) is int and row == 0):
                        pool.wait_ge(stored[tt], DMA * row)
                    pool.tensor_tensor(result[:, tt, :], x_sb[:, tt, :], rows["out1"][:, :], ALU.add
                                       ).then_inc(result_biased, 1)

            pool.memset(minus_half[:, :], -0.5).then_inc(const_set, 1)
            pool.wait_ge(const_set, 1)
            inverse_deviation("y0", 0)
            low_of_silu(0)
            pool.wait_ge(rows_in, 4 * DMA)
            bias_x(0)
            inverse_deviation("x1", 0)
            pool.wait_ge(bias_made, 3)
            pool.memset(att_bd[:, :, :], 0.0).then_inc(const_set, 1)

            def iteration(kind, b):
                if kind != "first":
                    inverse_deviation("y1", b - 1)
                    low_of_silu(KT * 2 * b)
                if kind != "last":
                    inverse_deviation("y0", b + 1)
                bias_result(b, range(0, 3))
                if kind != "last":
                    low_of_silu(KT * (2 * b + 1))
                bias_result(b, range(3, TT))
                if kind != "last":
                    bias_x(b + 1)
                for tt in range(TT):
                    if tt == 2 and kind != "last":
                        inverse_deviation("x1", b + 1)
                    pool.wait_ge(q_max_done, TT * b + tt + 1)
                    q = q_sb[:, tt, :].rearrange("p (h d) -> p h d", h=H1)
                    pool.tensor_tensor(q, q, qmax[:, tt, :].unsqueeze(2).broadcast_to([P, H1, DH1]), ALU.add
                                       ).then_inc(q_shifted, 1)

            iteration("first", 0)
            with pool.Fori(1, B - 1) as b:
                iteration("mid", b)
            iteration("last", B - 1)
            inverse_deviation("y1", B - 1)
            low_of_silu(KT * (2 * B - 1))

        @block.vector
        def _(dve):
            def full(u):
                dve.wait_ge(work_full, u[1] + 1)

            def read(u):
                return bank_read[u[0] % RING]

            def statistics(n, row, src, write, written):
                write(0)
                for tt in range(TT):
                    if tt < TT - 1:
                        write(tt + 1)
                    written(tt)
                    last = dve.bn_stats(stats[:, tt, :], src[:, tt, :])
                last.then_inc(ln_step[n], 1)
                dve.wait_ge(ln_step[n], 3 * row + 1)
                dve.memset(var_eps[n][:, :], EPS)
                for tt in range(TT):
                    last = dve.bn_aggr(mv[n][:, tt, :], stats[:, tt, :])
                last.then_inc(ln_step[n], 1)
                dve.wait_ge(ln_step[n], 3 * row + 2)
                dve.tensor_tensor(var_eps[n][:, :], mv[n][:, :, 1], var_eps[n][:, :], ALU.add).then_inc(ln_step[n], 1)

            def normalise(n, row, src, dst):
                dve.wait_ge(rstd_done[n], row + 1)
                for tt in range(TT):
                    dve.tensor_scalar(dst[:, tt, :], src[:, tt, :], mv[n][:, tt, 0:1], rstd[n][:, tt:tt + 1],
                                      ALU.subtract, ALU.mult).then_inc(hat_done[n], 1)

            def normalised_heads(kind, b, what, rec, split, order, n, row):
                def write(tt):
                    u = use(kind, b, what, tt)
                    full(u)
                    dve.tensor_tensor(yn[:, tt, :].rearrange(split, **order), bank(u).rearrange(split, **order),
                                      rec(tt), ALU.mult).then_inc(read(u), 1)

                statistics(n, row, yn, write, lambda tt: wait_read(dve, kind, b, what, tt))

            def A(kind, b, row):
                dve.wait_ge(sums_turned, row + 1)
                dve.reciprocal(rinv0[:, :, :], sums_bank[:, 0:TT * H0].rearrange("p (t h) -> p t h", t=TT)
                               ).then_inc(rinv0_done, 1)
                dve.wait_ge(rinv0_done, row + 1)
                normalised_heads(kind, b, "A",
                                 lambda tt: rinv0[:, tt, :].unsqueeze(2).broadcast_to([P, H0, DH0]),
                                 "p (h l) -> p h l", dict(h=H0), "y0", row)

            def Y(kind, b):
                dve.wait_ge(qrec_done, b + 1)
                normalised_heads(kind, b, "Y",
                                 lambda tt: qrec[:, tt, :].unsqueeze(2).broadcast_to([P, H1, DH1]),
                                 "p (h d) -> p h d", dict(h=H1), "y1", b)

            def highs_of_silu(kind, b, what):
                for kt in range(KT):
                    wait_read(dve, kind, b, what, kt)
                    dve.tensor_copy(sT_hi[:, kt, :], silu[:, kt % SILUS, :]).then_inc(sT_hi_done, 1)

            def C(kind, b, row):
                def write(tt):
                    dve.wait_ge(x_biased, TT * row + tt + 1)
                    u = use(kind, b, "C", tt)
                    full(u)
                    dve.tensor_tensor(x_sb[:, tt, :], bank(u), x_sb[:, tt, :], ALU.add).then_inc(read(u), 1)

                statistics("x1", row, x_sb, write, lambda tt: wait_read(dve, kind, b, "C", tt))

            def X(kind, b, row, kt):
                u = use(kind, b, "X", kt)
                dve.wait_ge(x1T_hi_done, KT * row + kt + 1)
                dve.tensor_tensor(x1T_lo[:, kt, :], bank(u), x1T_hi[:, kt, :].bitcast(F32), ALU.subtract
                                  ).then_inc(read(u), 1)

            def k_tile(kind, b, g):
                u = use(kind, b, "K", g)
                full(u)
                dve.scalar_tensor_tensor(out=ekT[:, g, :], in0=bank(u), scalar=k_bias[:, g:g + 1],
                                         in1=mask_bias[:, :], op0=ALU.add, op1=ALU.add).then_inc(read(u), 1)

            def k_max(kind, b, g):
                wait_read(dve, kind, b, "K", g)
                dve.tensor_reduce(kmax[:, g:g + 1], ekT[:, g, :], AXX, ALU.max, negate=True).then_inc(k_max_done, 1)

            def q_tile(kind, b, tt):
                u = use(kind, b, "Q", tt)
                full(u)
                dve.tensor_tensor(q_sb[:, tt, :], bank(u), rows["q"][:, :], ALU.add).then_inc(read(u), 1)

            def q_max(kind, b, tt):
                wait_read(dve, kind, b, "Q", tt)
                dve.tensor_reduce(qmax[:, tt, :], q_sb[:, tt, :].rearrange("p (h d) -> p h d", h=H1), AXX, ALU.max,
                                  negate=True).then_inc(q_max_done, 1)

            def add_row(kind, b, what, tt, dst, row):
                u = use(kind, b, what, tt)
                full(u)
                dve.tensor_tensor(dst[:, tt, :], bank(u), row, ALU.add).then_inc(read(u), 1)

            def add_result(kind, b, row):
                for tt in range(TT):
                    dve.wait_ge(result_biased, TT * row + tt + 1)
                    add_row(kind, b, "M", tt, result, result[:, tt, :])

            def low_of_w(n):
                low_of_weight(dve, w_raw[n], None if n in ("out0", "out1") else shared.lnw, w_hi[n], w_lo[n],
                              w_hi_done[n], w_split)

            dve.tensor_copy(lnb_rep[:, :, :], shared.lnb.unsqueeze(2).broadcast_to([P, KT, P])).then_inc(lnb_rep_done, 1)
            A("start", 0, 0)
            low_of_w("out0")
            normalise("y0", 0, yn, yn)
            dve.wait_ge(bias_made, 1)
            dve.tensor_tensor(k_bias[:, :], sums_bank[:, 0:NG], shared.k_b, ALU.add).then_inc(bias_done, 1)
            highs_of_silu("start", 0, "S")
            low_of_w("k")
            low_of_w("v")
            C("start", 0, 0)
            low_of_w("q")
            normalise("x1", 0, x_sb, x1hat)
            for kt in range(KT):
                X("start", 0, 0, kt)
            low_of_w("out1")
            dve.wait_ge(rows_in, 4 * DMA)
            for i, n in enumerate("vq"):
                dve.wait_ge(bias_made, 2 + i)
                dve.tensor_tensor(rows[n][:, :], (att_bank, sums_bank)[i][:, :], rows[n][:, :], ALU.add).then_inc(bias_done, 1)
            dve.wait_ge(bias_done, 3)

            def iteration(kind, b):
                dve.wait_ge(mask_bias_in, DMA * (b + 1))
                k_tile(kind, b, 0)
                k_tile(kind, b, 1)
                k_max(kind, b, 0)
                if kind != "first":
                    normalise("y1", b - 1, yn, yn)
                for g in range(2, NG):
                    k_tile(kind, b, g)
                    k_max(kind, b, g - 1)
                k_max(kind, b, NG - 1)
                if kind != "first":
                    highs_of_silu(kind, b, "L")
                if kind != "last":
                    A(kind, b, b + 1)
                add_row(kind, b, "V", 0, v_sb, rows["v"][:, :])
                add_row(kind, b, "V", 1, v_sb, rows["v"][:, :])
                if kind != "last":
                    normalise("y0", b + 1, yn, yn)
                add_row(kind, b, "V", 2, v_sb, rows["v"][:, :])
                add_row(kind, b, "V", 3, v_sb, rows["v"][:, :])
                if kind != "first":
                    add_result(kind, b, b - 1)
                if kind != "last":
                    highs_of_silu(kind, b, "S")
                dve.wait_ge(k_exp_done, NG * (b + 1))
                dve.reciprocal(krec[:, :], ksum[:, :]).then_inc(krec_done, 1)
                q_tile(kind, b, 0)
                q_tile(kind, b, 1)
                q_max(kind, b, 0)
                q_max(kind, b, 1)
                if kind != "last":
                    C(kind, b, b + 1)
                q_tile(kind, b, 2)
                q_max(kind, b, 2)
                q_tile(kind, b, 3)
                q_max(kind, b, 3)
                if kind != "last":
                    normalise("x1", b + 1, x_sb, x1hat)
                dve.wait_ge(att_made, b + 1)
                dve.wait_ge(krec_done, b + 1)
                for half in range(2):
                    at = slice(DH1 * half, DH1 * (half + 1))
                    last = dve.tensor_tensor(att_bd[at, :, at], att_bank[at, :].rearrange("p (k c) -> p k c", k=KT)[:, :, at],
                                             krec[at, :].unsqueeze(2).broadcast_to([DH1, KT, DH1]), ALU.mult)
                last.then_inc(att_done, 1)
                for tt in range(TT):
                    if kind != "last":
                        X(kind, b, b + 1, tt)
                    dve.wait_ge(q_exp_done, TT * b + tt + 1)
                    last = dve.tensor_reduce(qsum[:, tt, :], q_sb[:, tt, :].rearrange("p (h d) -> p h d", h=H1), AXX, ALU.add)
                last.then_inc(q_sum_done, 1)
                dve.wait_ge(q_sum_done, b + 1)
                dve.reciprocal(qrec[:, :, :], qsum[:, :, :]).then_inc(qrec_done, 1)
                Y(kind, b)

            dve.wait_ge(const_set, 2)
            iteration("first", 0)
            with dve.Fori(1, B - 1) as b:
                iteration("mid", b)
            iteration("last", B - 1)
            normalise("y1", B - 1, yn, yn)
            highs_of_silu("end", B - 1, "L")
            add_result("end", B - 1, B - 1)


_NAMES = ["x", "cond_2048", "mask_BxS_ff1", "mask_BxSx1_fk1", "L0_cond_norm_w", "L0_cond_norm_b", "L0_cond_q_w",
          "L0_cond_q_b", "L0_cond_k_w", "L0_cond_k_b", "L0_cond_v_w", "L0_cond_v_b", "L0_cond_emb_w", "L0_cond_emb_b",
          "L0_cond_sb_norm_w", "L0_cond_sb_norm_b", "L0_cond_out_w", "L0_cond_out_b", "L1_cond_ln_w", "L1_cond_ln_b",
          "L1_cond_Wq", "L1_cond_bq", "L1_cond_Wk", "L1_cond_bk", "L1_cond_Wv", "L1_cond_bv", "L1_cond_W_emb",
          "L1_cond_b_emb", "L1_cond_ln2_w", "L1_cond_ln2_b", "L1_cond_W_out", "L1_cond_b_out"]


def build(nc, i, out):
    B = i["x"].shape[0]
    yT_dram = nc.dram_tensor("yT_scratch", (B, D, T), F32, kind="Internal").ap()
    sums_dram = nc.dram_tensor("sums_scratch", (B, NG * HG, T), F32, kind="Internal").ap()
    mb0_dram = nc.dram_tensor("mask_bias0_scratch", (B, 2, T), F32, kind="Internal").ap()
    mb1_dram = nc.dram_tensor("mask_bias1_scratch", (B, T), F32, kind="Internal").ap()
    mask1 = i["mask_BxSx1_fk1"].rearrange("b t o -> b (t o)")
    films = [tuple(i[layer + n] for n in names) for layer, names in
             (("L0_cond_", ("emb_w", "emb_b", "sb_norm_w", "sb_norm_b")), ("L1_cond_", ("W_emb", "b_emb", "ln2_w", "ln2_b")))]
    b_vectors = films[0][1:] + films[1][1:] + (i["L1_cond_ln_w"], i["L1_cond_ln_b"], i["L1_cond_bk"])
    with ExitStack() as ctx:
        shared = Shared(nc, ctx, B)
        attention_phase(nc, shared, i["x"], i["mask_BxS_ff1"], mask1, i["L0_cond_norm_w"], i["L0_cond_norm_b"],
                        i["L0_cond_q_w"], i["L0_cond_q_b"], i["L0_cond_k_w"], i["L0_cond_k_b"], i["L0_cond_v_w"],
                        i["L0_cond_v_b"], i["cond_2048"], [film[0] for film in films], b_vectors,
                        yT_dram, sums_dram, mb0_dram, mb1_dram)
        projection_phase(nc, shared, i["x"], i["L0_cond_out_w"], i["L0_cond_out_b"], i["L1_cond_Wq"], i["L1_cond_bq"],
                         i["L1_cond_Wk"], i["L1_cond_Wv"], i["L1_cond_bv"], i["L1_cond_W_out"], i["L1_cond_b_out"],
                         yT_dram, sums_dram, mb1_dram, out)


def kernel(**inputs):
    import concourse.bacc as bacc
    import numpy as np
    from concourse.bass_utils import run_bass_kernel_spmd

    nc = bacc.Bacc("TRN2", target_bir_lowering=False, num_devices=1)
    arrays, aps = {}, {}
    for name in _NAMES:
        a = np.ascontiguousarray(inputs[name])
        arrays[f"in_{name}"] = a
        aps[name] = nc.dram_tensor(f"in_{name}", a.shape, mybir.dt.from_np(a.dtype), kind="ExternalInput").ap()
    out = nc.dram_tensor("out_x", arrays["in_x"].shape, F32, kind="ExternalOutput").ap()
    build(nc, aps, out)
    r = run_bass_kernel_spmd(nc, [arrays], core_ids=[0])
    return r.results[0]["out_x"]
```
